# Optimizing a Trainium2 kernel written in Bass

```python
import numpy as np
import jax
import jax.numpy as jnp

def _softmax(x, axis=-1):
    return jax.nn.softmax(x, axis=axis)

def _gelu(x):
    return jax.nn.gelu(x, approximate=True)

def _silu(x):
    return jax.nn.silu(x)

def _sigmoid(x):
    return jax.nn.sigmoid(x)

def _layernorm(x, axis=-1, eps=1e-05):
    m = jnp.mean(x, axis=axis, keepdims=True)
    v = jnp.var(x, axis=axis, keepdims=True)
    return (x - m) / jnp.sqrt(v + eps)

def _scatter_add(tgt, idx, src, axis=0):
    return tgt.at[idx].add(src)

def _segment_sum(src, seg, n):
    return jax.ops.segment_sum(src, seg, n)
kernel_name = 'mk_gnn_ffn_d1_gnn_r8_c8ba6a'

def setup_inputs(seed: int=0):
    np.random.seed(seed)
    _w = jnp.asarray

    def _rec_inputs():
        import jax
        import jax.numpy as jnp
        _gk = jax.random.key(seed)
        x = -0.0005963 + 1.001 * jax.random.normal(jax.random.fold_in(_gk, 1), (384, 1024), jnp.float32)
        src = jax.random.randint(jax.random.fold_in(_gk, 2), (6144,), 0, 384, jnp.int32)
        dst = jax.random.randint(jax.random.fold_in(_gk, 3), (6144,), 0, 384, jnp.int32)
        _o = jnp.argsort(dst, stable=True)
        src = src[_o]
        dst = dst[_o]
        edge_type_5 = jax.random.randint(jax.random.fold_in(_gk, 12), (6144,), 0, 5, jnp.int32)
        return (x, src, dst, edge_type_5)
    x, src, dst, edge_type_5 = _rec_inputs()

    def _L0_gnn_setup():
        import jax, jax.numpy as jnp
        import numpy as np
        N = 384
        E = 12288
        IN_F = 1024
        OUT_F = 1024
        H = 16
        D = OUT_F // H
        NUM_ETYPES = 4

        def _build_mask(edge_index, edge_type, edge_type_weights, dtype):
            src, dst = (edge_index[0], edge_index[1])
            w = jax.nn.softplus(edge_type_weights)
            mask = jnp.full((N, N), -jnp.inf, dtype=dtype)
            mask = mask.at[src, dst].set(w[edge_type - 1])
            diag = jnp.diagonal(mask)
            idx = jnp.arange(N)
            mask = mask.at[idx, idx].set(jnp.where(jnp.isneginf(diag), w[3], diag))
            return mask
        key = jax.random.key(seed)
        ks = jax.random.split(key, 20)
        p = lambda k, shape: jax.random.normal(k, shape, dtype=jnp.float32) * 0.02
        return {'x': jax.random.normal(ks[0], (N, IN_F), dtype=jnp.float32), 'edge_index': jax.random.randint(ks[1], (2, E), 0, N), 'edge_type': jax.random.randint(ks[2], (E,), 1, NUM_ETYPES + 1), 'edge_type_weights': jnp.ones((NUM_ETYPES,), jnp.float32) + 0.1 * jax.random.normal(ks[3], (NUM_ETYPES,), dtype=jnp.float32), 'wq': p(ks[4], (OUT_F, IN_F)), 'bq': p(ks[5], (OUT_F,)), 'wk': p(ks[6], (OUT_F, IN_F)), 'bk': p(ks[7], (OUT_F,)), 'wv': p(ks[8], (OUT_F, IN_F)), 'bv': p(ks[9], (OUT_F,)), 'wiq': p(ks[10], (OUT_F, OUT_F)), 'biq': p(ks[11], (OUT_F,)), 'wik': p(ks[12], (OUT_F, OUT_F)), 'bik': p(ks[13], (OUT_F,)), 'wiv': p(ks[14], (OUT_F, OUT_F)), 'biv': p(ks[15], (OUT_F,)), 'wo': p(ks[16], (OUT_F, OUT_F)), 'bo': p(ks[17], (OUT_F,))}
    _L0_gnn_all = _L0_gnn_setup()
    _L0_gnn_in = {k: v for k, v in _L0_gnn_all.items() if k in ('edge_type_weights', 'wq', 'bq', 'wk', 'bk', 'wv', 'bv', 'wiq', 'biq', 'wik', 'bik', 'wiv', 'biv', 'wo', 'bo')}
    del _L0_gnn_all

    def _L0_ffn_setup():
        import jax, jax.numpy as jnp
        import numpy as np
        B, S, D = (1, 256, 1024)
        E, F = (16, 1024)
        NG, TKG, K = (4, 2, 4)
        NSH = 2
        SCALE = 2.5
        STD = 0.02
        EPG = E // NG

        def _route(x_flat, router_w, bias):
            logits = x_flat.astype(jnp.float32) @ router_w.T
            scores = jax.nn.sigmoid(logits)
            s = scores + bias[None, :]
            sg = s.reshape(-1, NG, EPG)
            group_score = jax.lax.top_k(sg, 2)[0].sum(-1)
            gidx = jax.lax.top_k(group_score, TKG)[1]
            gmask = jnp.sum(jax.nn.one_hot(gidx, NG, dtype=jnp.float32), axis=1) > 0
            emask = jnp.repeat(gmask, EPG, axis=1)
            masked = jnp.where(emask, s, -1.0)
            topk_idx = jax.lax.top_k(masked, K)[1]
            tw = jnp.take_along_axis(scores, topk_idx, axis=1)
            tw = tw / (tw.sum(-1, keepdims=True) + 1e-20)
            tw = tw * SCALE
            return (topk_idx, tw)
        key = jax.random.key(seed)
        ks = jax.random.split(key, 8)
        return {'hidden_states': jax.random.normal(ks[0], (B, S, D), jnp.float32), 'router_w': jax.random.normal(ks[1], (E, D), jnp.float32) * STD, 'bias': jnp.zeros((E,), jnp.float32), 'gate_w': jax.random.normal(ks[2], (E, D, F), jnp.float32) * STD, 'up_w': jax.random.normal(ks[3], (E, D, F), jnp.float32) * STD, 'down_w': jax.random.normal(ks[4], (E, F, D), jnp.float32) * STD, 'sh_gate_w': jax.random.normal(ks[5], (D, NSH * F), jnp.float32) * STD, 'sh_up_w': jax.random.normal(ks[6], (D, NSH * F), jnp.float32) * STD, 'sh_down_w': jax.random.normal(ks[7], (NSH * F, D), jnp.float32) * STD}
    _L0_ffn_all = _L0_ffn_setup()
    _L0_ffn_in = {k: v for k, v in _L0_ffn_all.items() if k in ('router_w', 'bias', 'gate_w', 'up_w', 'down_w', 'sh_gate_w', 'sh_up_w', 'sh_down_w')}
    del _L0_ffn_all
    return {'x': x, 'src': src, 'dst': dst, 'edge_type_5': edge_type_5, 'L0_gnn_edge_type_weights': _L0_gnn_in['edge_type_weights'], 'L0_gnn_wq': _L0_gnn_in['wq'], 'L0_gnn_bq': _L0_gnn_in['bq'], 'L0_gnn_wk': _L0_gnn_in['wk'], 'L0_gnn_bk': _L0_gnn_in['bk'], 'L0_gnn_wv': _L0_gnn_in['wv'], 'L0_gnn_bv': _L0_gnn_in['bv'], 'L0_gnn_wiq': _L0_gnn_in['wiq'], 'L0_gnn_biq': _L0_gnn_in['biq'], 'L0_gnn_wik': _L0_gnn_in['wik'], 'L0_gnn_bik': _L0_gnn_in['bik'], 'L0_gnn_wiv': _L0_gnn_in['wiv'], 'L0_gnn_biv': _L0_gnn_in['biv'], 'L0_gnn_wo': _L0_gnn_in['wo'], 'L0_gnn_bo': _L0_gnn_in['bo'], 'L0_ffn_router_w': _L0_ffn_in['router_w'], 'L0_ffn_bias': _L0_ffn_in['bias'], 'L0_ffn_gate_w': _L0_ffn_in['gate_w'], 'L0_ffn_up_w': _L0_ffn_in['up_w'], 'L0_ffn_down_w': _L0_ffn_in['down_w'], 'L0_ffn_sh_gate_w': _L0_ffn_in['sh_gate_w'], 'L0_ffn_sh_up_w': _L0_ffn_in['sh_up_w'], 'L0_ffn_sh_down_w': _L0_ffn_in['sh_down_w']}

def reference(x, src, dst, edge_type_5, L0_gnn_edge_type_weights, L0_gnn_wq, L0_gnn_bq, L0_gnn_wk, L0_gnn_bk, L0_gnn_wv, L0_gnn_bv, L0_gnn_wiq, L0_gnn_biq, L0_gnn_wik, L0_gnn_bik, L0_gnn_wiv, L0_gnn_biv, L0_gnn_wo, L0_gnn_bo, L0_ffn_router_w, L0_ffn_bias, L0_ffn_gate_w, L0_ffn_up_w, L0_ffn_down_w, L0_ffn_sh_gate_w, L0_ffn_sh_up_w, L0_ffn_sh_down_w):
    import jax
    import jax.numpy as jnp

    def _L0_gnn_ref(x, edge_index, edge_type, edge_type_weights, wq, bq, wk, bk, wv, bv, wiq, biq, wik, bik, wiv, biv, wo, bo):
        import jax, jax.numpy as jnp
        import numpy as np
        N = 384
        E = 12288
        IN_F = 1024
        OUT_F = 1024
        H = 16
        D = OUT_F // H
        NUM_ETYPES = 4

        def _build_mask(edge_index, edge_type, edge_type_weights, dtype):
            src, dst = (edge_index[0], edge_index[1])
            w = jax.nn.softplus(edge_type_weights)
            mask = jnp.full((N, N), -jnp.inf, dtype=dtype)
            mask = mask.at[src, dst].set(w[edge_type - 1])
            diag = jnp.diagonal(mask)
            idx = jnp.arange(N)
            mask = mask.at[idx, idx].set(jnp.where(jnp.isneginf(diag), w[3], diag))
            return mask
        q = x @ wq.T + bq
        k = x @ wk.T + bk
        v = x @ wv.T + bv
        q2 = (q @ wiq.T + biq).reshape(N, H, D).transpose(1, 0, 2)
        k2 = (k @ wik.T + bik).reshape(N, H, D).transpose(1, 0, 2)
        v2 = (v @ wiv.T + biv).reshape(N, H, D).transpose(1, 0, 2)
        mask = _build_mask(edge_index, edge_type, edge_type_weights, x.dtype)
        scale = 1.0 / np.sqrt(D).astype(np.float32)
        scores = jnp.einsum('hnd,hmd->hnm', q2, k2) * scale + mask[None]
        attn = jax.nn.softmax(scores, axis=-1)
        out = jnp.einsum('hnm,hmd->hnd', attn, v2)
        out = out.transpose(1, 0, 2).reshape(N, OUT_F)
        return out @ wo.T + bo

    def _L0_ffn_ref(hidden_states, router_w, bias, gate_w, up_w, down_w, sh_gate_w, sh_up_w, sh_down_w):
        import jax, jax.numpy as jnp
        import numpy as np
        B, S, D = (1, 256, 1024)
        E, F = (16, 1024)
        NG, TKG, K = (4, 2, 4)
        NSH = 2
        SCALE = 2.5
        STD = 0.02
        EPG = E // NG

        def _route(x_flat, router_w, bias):
            logits = x_flat.astype(jnp.float32) @ router_w.T
            scores = jax.nn.sigmoid(logits)
            s = scores + bias[None, :]
            sg = s.reshape(-1, NG, EPG)
            group_score = jax.lax.top_k(sg, 2)[0].sum(-1)
            gidx = jax.lax.top_k(group_score, TKG)[1]
            gmask = jnp.sum(jax.nn.one_hot(gidx, NG, dtype=jnp.float32), axis=1) > 0
            emask = jnp.repeat(gmask, EPG, axis=1)
            masked = jnp.where(emask, s, -1.0)
            topk_idx = jax.lax.top_k(masked, K)[1]
            tw = jnp.take_along_axis(scores, topk_idx, axis=1)
            tw = tw / (tw.sum(-1, keepdims=True) + 1e-20)
            tw = tw * SCALE
            return (topk_idx, tw)
        x = hidden_states.reshape(-1, D)
        topk_idx, tw = _route(x, router_w, bias)
        combine = (jax.nn.one_hot(topk_idx, E, dtype=tw.dtype) * tw[..., None]).sum(1)
        h = jnp.einsum('td,edf->etf', x, gate_w)
        u = jnp.einsum('td,edf->etf', x, up_w)
        y = jnp.einsum('etf,efd->etd', jax.nn.silu(h) * u, down_w)
        routed = jnp.einsum('etd,te->td', y, combine)
        sh = jax.nn.silu(x @ sh_gate_w) * (x @ sh_up_w) @ sh_down_w
        return (routed + sh).reshape(hidden_states.shape)
    edge_index = jnp.stack([src, dst])
    x = x + _L0_gnn_ref(_layernorm(x, axis=-1), edge_index, edge_type_5, L0_gnn_edge_type_weights, L0_gnn_wq, L0_gnn_bq, L0_gnn_wk, L0_gnn_bk, L0_gnn_wv, L0_gnn_bv, L0_gnn_wiq, L0_gnn_biq, L0_gnn_wik, L0_gnn_bik, L0_gnn_wiv, L0_gnn_biv, L0_gnn_wo, L0_gnn_bo)
    x = x + _L0_ffn_ref(_layernorm(x, axis=-1)[None], L0_ffn_router_w, L0_ffn_bias, L0_ffn_gate_w, L0_ffn_up_w, L0_ffn_down_w, L0_ffn_sh_gate_w, L0_ffn_sh_up_w, L0_ffn_sh_down_w)[0]
    return x

_drawn_inputs = setup_inputs


def setup_inputs(seed=0):
    import zlib

    import numpy as np

    out = dict(_drawn_inputs(seed))
    spreads = {'L0_ffn_bias': (0.0, 0.1)}
    factors = {'L0_gnn_edge_type_weights': 3.87,
     'L0_gnn_wq': 2.988,
     'L0_gnn_bq': 8.0,
     'L0_gnn_wk': 2.908,
     'L0_gnn_bk': 8.0,
     'L0_gnn_bv': 3.981,
     'L0_gnn_wiq': 3.44,
     'L0_gnn_biq': 8.0,
     'L0_gnn_wik': 3.354,
     'L0_gnn_bik': 8.0}
    for name, (base, spread) in spreads.items():
        noise = np.random.default_rng([zlib.crc32(name.encode()), seed]).standard_normal(out[name].shape)
        drawn = base * np.exp(spread * noise) if base else spread * noise
        out[name] = jnp.asarray(drawn.astype(out[name].dtype))
    for name, factor in factors.items():
        out[name] = (out[name] * factor).astype(out[name].dtype)
    return out
```

```python
from contextlib import ExitStack

import numpy as np
import concourse.bass as bass
from concourse import mybir
from concourse.alu_op_type import AluOpType as ALU

F32 = mybir.dt.float32
F32R = mybir.dt.float32r
BF16 = mybir.dt.bfloat16
I32 = mybir.dt.int32
ACT = mybir.ActivationFunctionType
AX = mybir.AxisListType

P = 128
N = 384
NT = N // P
D = 1024
KT = D // P
HEADS = 16
DH = D // HEADS
EDGES = 6144
EC = EDGES // P
SUPER = 8
NS = EC // SUPER
EXPERTS = 16
GROUPS = 4
GSIZE = EXPERTS // GROUPS
SHARED = 2
ROUTE_SCALE = 2.5
EPS = 1e-5
ABSENT = -1.0e30

HALF = 512
KPIECE = 4
RAW = 4
SPLIT = 3


class Lane:

    def __init__(self, sem):
        self.sem, self.count, self.steps, self.waited = sem, 0, [], {}

    def wait(self, *tokens):
        for sem, value in tokens:
            if self.waited.get(id(sem), 0) < value:
                self.waited[id(sem)] = value
                self.steps.append(lambda e, s=sem, v=value: e.wait_ge(s, v))

    def run(self, step):
        self.steps.append(step)

    def do(self, step):
        self.count += 1
        self.steps.append(lambda e: step(e).then_inc(self.sem, 1))
        return self.sem, self.count

    def chain(self, step):
        done = self.do(step)
        self.wait(done)
        return done

    def emit(self, engine):
        for step in self.steps:
            step(engine)


class Arrival:

    def __init__(self, sem):
        self.sem, self.count = sem, 0

    def load(self, lane, out, in_):
        self.count += 16
        lane.run(lambda e: e.dma_start(out, in_).then_inc(self.sem, 16))
        return self.sem, self.count


def build(nc, A, out):
    with ExitStack() as ctx, ExitStack() as gnn_buffers:
        def sb(name, shape, dt=F32, scope=ctx):
            return scope.enter_context(nc.sbuf_tensor(name, shape, dt))

        def sem(name):
            return ctx.enter_context(nc.semaphore(name))

        bank = [ctx.enter_context(nc.psum_tensor(f"bank{i}", [P, HALF], F32)) for i in range(8)]
        bank_read = [None] * 8

        raw = sb("raw", [P, RAW, KPIECE, HALF])
        w_hi = sb("w_hi", [P, SPLIT, KPIECE, HALF], F32R)
        w_lo = sb("w_lo", [P, SPLIT, KPIECE, HALF], F32R)
        in_hi = sb("in_hi", [P, KT, N], F32R)
        in_lo = sb("in_lo", [P, KT, N], F32R)
        x_rows = sb("x_rows", [P, NT, D])
        ident = sb("ident", [P, P])
        stats = sb("stats", [P, NT, 2, 6])
        meanvar = sb("meanvar", [P, NT, 2])
        rstd = sb("rstd", [P, NT])
        half_neg = sb("half_neg", [P, NT])
        row_bias = sb("row_bias", [P, D])
        cols = sb("cols", [P, 5, KT])

        g = gnn_buffers
        mid_hi = sb("mid_hi", [P, KT, N], F32R, g)
        mid_lo = sb("mid_lo", [P, KT, N], F32R, g)
        q2 = sb("q2", [P, KT, N], F32, g)
        rows = q2[:].rearrange("p k n -> p (k n)").rearrange("p (t d) -> p t d", t=NT)
        k2 = sb("k2", [P, KT, N], F32, g)
        mask8 = sb("mask8", [P, NT, N], F32, g)
        sums = sb("sums", [P, 4, 2], F32, g)
        etw = sb("etw", [P, 6, 4], F32, g)
        with ExitStack() as edge_buffers:
            b = edge_buffers
            src_row = sb("src_row", [P, SUPER * P], I32, b)
            dst_row = sb("dst_row", [P, SUPER * P], I32, b)
            key_row = sb("key_row", [P, SUPER * P], F32, b)
            later = sb("later", [P, SUPER * P], BF16, b)
            same = sb("same", [P, SUPER * P], BF16, b)
            onehot_src = sb("onehot_src", [P, 2, N], BF16, b)
            onehot_dst = sb("onehot_dst", [P, 2, N], BF16, b)
            node = sb("node", [P, N], F32, b)
            diag = sb("diag", [P, NT, N], F32, b)
            ecol_i = sb("ecol_i", [P, 3, EC], I32, b)
            ecol = sb("ecol", [P, 8, EC], F32, b)
        with ExitStack() as attention_buffers:
            b = attention_buffers
            v2 = sb("v2", [P, NT, D], F32, b)
            score = sb("score", [P, 2, N], F32, b)
            prob = sb("prob", [P, 3, N], F32, b)
            prob_t = sb("prob_t", [P, 2, NT, N], F32, b)
        gnn_buffers.close()

        act_hi = sb("act_hi", [P, KT, N], F32R)
        act_lo = sb("act_lo", [P, KT, N], F32R)
        rows2 = sb("rows2", [P, NT, D])
        gated = sb("gated", [P, NT, HALF])
        hidden = sb("hidden", [P, 2, HALF])
        router_raw = sb("router_raw", [P, KT, EXPERTS])
        router_hi = sb("router_hi", [P, KT, EXPERTS], F32R)
        router_lo = sb("router_lo", [P, KT, EXPERTS], F32R)
        e_bias = sb("e_bias", [P, EXPERTS])
        prob_e = sb("prob_e", [P, NT, EXPERTS])
        r = [sb(f"route{i}", [P, NT, EXPERTS]) for i in range(4)]
        gs = sb("gs", [P, NT, 6, GROUPS])
        beats = sb("beats", [P, EXPERTS, EXPERTS])
        beats2 = sb("beats2", [P, EXPERTS, EXPERTS])
        earlier = sb("earlier", [P, EXPERTS, EXPERTS])
        combine = sb("combine", [P, NT, EXPERTS])
        denom = sb("denom", [P, NT])

        pe, act, dve, pool = (Lane(sem(f"{n}_done")) for n in ("tensor", "scalar", "vector", "gpsimd"))
        sync = Lane(None)
        raw_in = [Arrival(sem(f"raw_in{i}")) for i in range(RAW)]

        pieces = []
        raw_free = [None] * RAW
        split_free = [None] * SPLIT

        def matrix(w, halves=(0, 1)):
            return [w.rearrange("(k p) f -> p k f", p=P)[:, kh * KPIECE:(kh + 1) * KPIECE,
                                                         c * HALF:(c + 1) * HALF]
                    for c in halves for kh in range(KT // KPIECE)]

        for w in ("wq", "wiq", "wk", "wik", "wv", "wiv", "wo"):
            pieces += matrix(A[w])

        def unit_matrices(u):
            if u < SHARED:
                cut = slice(u * D, (u + 1) * D)
                return A["sh_gate"][:, cut], A["sh_up"][:, cut], A["sh_down"][cut, :]
            return A["gate"][u - SHARED], A["up"][u - SHARED], A["down"][u - SHARED]

        UNITS = SHARED + EXPERTS
        for u in range(UNITS):
            gate, up, down = unit_matrices(u)
            for c in range(2):
                pieces += matrix(gate, (c,)) + matrix(up, (c,))
            pieces += matrix(down)

        loaded, taken = [], [0]

        def load_ahead(upto):
            while len(loaded) < min(upto, len(pieces)):
                i = len(loaded)
                s = i % RAW
                if raw_free[s]:
                    sync.wait(raw_free[s])
                loaded.append(raw_in[s].load(sync, raw[:, s], pieces[i]))

        def next_piece():
            i = taken[0]
            taken[0] += 1
            load_ahead(i + 1)
            s, t = i % RAW, i % SPLIT
            act.wait(loaded[i])
            if split_free[t]:
                act.wait(split_free[t])
            hi = act.do(lambda e: e.activation(w_hi[:, t], raw[:, s], ACT.Copy))
            dve.wait(hi)
            lo = dve.do(lambda e: e.tensor_tensor(w_lo[:, t], raw[:, s], w_hi[:, t].bitcast(F32),
                                                  ALU.subtract))
            raw_free[s] = lo
            load_ahead(i + 1 + RAW)
            return t, (hi, lo)

        def piece_done(t, done):
            split_free[t] = done

        PASSES = ((0, 0), (1, 0), (0, 1))

        def product_rows(source, evacuate, banks, tiles=range(NT), behind=()):
            for kh in range(KT // KPIECE):
                t, ready = next_piece()
                pe.wait(*ready)
                for i in tiles:
                    bk = banks[i]
                    if kh == 0 and bank_read[bk]:
                        pe.wait(bank_read[bk])
                    for n in range(KPIECE):
                        k = kh * KPIECE + n
                        for m, (a, w) in enumerate(PASSES):
                            first, last = k == 0 and m == 0, k == KT - 1 and m == 2
                            step = (lambda e, bk=bk, k=k, i=i, a=a, w=w, n=n, t=t, first=first, last=last:
                                    e.matmul(bank[bk][:], source[a][:, k, i * P:(i + 1) * P],
                                             (w_hi, w_lo)[w][:, t, n], start=first, stop=last))
                            if n == KPIECE - 1 and m == 2:
                                done = pe.do(step)
                            else:
                                pe.run(step)
                    if kh == KT // KPIECE - 1:
                        bank_read[bk] = evacuate(i, bk, done)
                piece_done(t, done)
                if kh == 0:
                    for work in behind:
                        work()

        turn = [0]

        def product_cols(source, c, evacuate):
            ring = (3, 4, 5, 6, 7)
            banks = [ring[(turn[0] + m) % 5] for m in range(4)]
            turn[0] += 4
            for kh in range(KT // KPIECE):
                t, ready = next_piece()
                pe.wait(*ready)
                for f in range(HALF // P):
                    bk = banks[f]
                    if kh == 0 and bank_read[bk]:
                        pe.wait(bank_read[bk])
                    for n in range(KPIECE):
                        k = kh * KPIECE + n
                        for m, (a, w) in enumerate(PASSES):
                            first, last = k == 0 and m == 0, k == KT - 1 and m == 2
                            step = (lambda e, bk=bk, k=k, f=f, a=a, w=w, n=n, t=t, first=first, last=last:
                                    e.matmul(bank[bk][:, 0:N], (w_hi, w_lo)[w][:, t, n, f * P:(f + 1) * P],
                                             source[a][:, k, :], start=first, stop=last))
                            if n == KPIECE - 1 and m == 2:
                                done = pe.do(step)
                            else:
                                pe.run(step)
                    if kh == KT // KPIECE - 1:
                        bank_read[bk] = evacuate(c * (HALF // P) + f, bk, done)
                piece_done(t, done)
                yield

        small = Arrival(sem("small_in"))
        for i, name in enumerate(("bq", "biq", "bk", "bik", "bv")):
            got_small = small.load(sync, cols[:, i, :], A[name])
        got_small = small.load(sync, x_rows[:], A["x"].rearrange("(t p) d -> p t d", p=P))
        for i, name in enumerate(("src_cols", "dst_cols", "type_cols")):
            got_small = small.load(sync, ecol_i[:, i, :], A[name])
        got_small = small.load(sync, etw[:, 0, :], A["etw"].partition_broadcast(P))
        load_ahead(RAW)

        row_in = Arrival(sem("edge_rows_in"))
        bias_in = Arrival(sem("bias_in"))
        biv_in = bias_in.load(sync, row_bias[:], A["biv"].partition_broadcast(P))

        zeroed = pool.do(lambda e: e.memset(ident[:], 0.0))
        pool.chain(lambda e: e.memset(diag[:], 0.0))
        have_ident = pool.do(lambda e: e.affine_select(out=ident[:], in_=ident[:], compare_op=ALU.not_equal,
                                                       fill=1.0, base=0, pattern=[[-1, P]],
                                                       channel_multiplier=1))
        have_diag = pool.do(lambda e: e.affine_select(out=diag[:], in_=diag[:], compare_op=ALU.not_equal,
                                                      fill=0.5, base=0, pattern=[[P, NT], [-1, N]],
                                                      channel_multiplier=1))
        have_node = pool.do(lambda e: e.iota(node[:], pattern=[[1, N]], base=0, channel_multiplier=0,
                                             allow_small_or_imprecise_dtypes=True))
        pool.chain(lambda e: e.memset(later[:], 1.0))
        have_later = pool.do(lambda e: e.affine_select(out=later[:], in_=later[:], compare_op=ALU.is_gt,
                                                       fill=0.0, base=0, pattern=[[1, SUPER * P]],
                                                       channel_multiplier=-1))
        have_half = pool.chain(lambda e: e.memset(half_neg[:], -0.5))

        def layer_norm(target, ready):
            dve.wait(ready)
            for i in range(NT):
                for hh in range(2):
                    stat = dve.do(lambda e, i=i, hh=hh: e.bn_stats(stats[:, i, hh, :],
                                                                   x_rows[:, i, hh * HALF:(hh + 1) * HALF]))
            dve.wait(stat)
            for i in range(NT):
                agg = dve.do(lambda e, i=i: e.bn_aggr(meanvar[:, i, :],
                                                      stats[:, i].rearrange("p a b -> p (a b)")))
            dve.wait(agg)
            var = dve.do(lambda e: e.tensor_scalar(rstd[:], meanvar[:, :, 1], EPS, None, ALU.add))
            pool.wait(var, have_half)
            power = pool.do(lambda e: e.tensor_tensor(rstd[:], rstd[:], half_neg[:], ALU.pow))
            dve.wait(power)
            done = []
            for i in range(NT):
                done.append(dve.do(lambda e, i=i: e.tensor_scalar(target[:, i, :], x_rows[:, i, :],
                                                                  meanvar[:, i, 0:1], rstd[:, i:i + 1],
                                                                  ALU.subtract, ALU.mult)))
            return done

        def split_out(bk, width, hi, lo, ready, bias=None):
            act.wait(ready)
            if bias is None:
                h = act.do(lambda e: e.activation(hi, bank[bk][:, 0:width], ACT.Copy))
                dve.wait(h)
                return dve.do(lambda e: e.tensor_tensor(lo, bank[bk][:, 0:width], hi.bitcast(F32), ALU.subtract))
            h = act.do(lambda e: e.activation(hi, bank[bk][:, 0:width], ACT.Identity, bias=bias))
            dve.wait(h)
            return dve.do(lambda e: e.scalar_tensor_tensor(lo, bank[bk][:, 0:width], bias, hi.bitcast(F32),
                                                           ALU.add, ALU.subtract))

        def transpose_rows(source, ready, banks):
            pe.wait(have_ident, *ready)
            for k in range(KT):
                bk = banks[k % len(banks)]
                if bank_read[bk]:
                    pe.wait(bank_read[bk])
                for i in range(NT):
                    done = pe.do(lambda e, i=i, k=k, bk=bk: e.transpose(
                        bank[bk][:, i * P:(i + 1) * P], source[:, i, k * P:(k + 1) * P], ident[:]))
                got = bank_read[bk] = split_out(bk, N, in_hi[:, k, :], in_lo[:, k, :], done)
            return got

        dve.wait(got_small)
        act.wait(got_small)
        dve.chain(lambda e: e.tensor_scalar(etw[:, 1, :], etw[:, 0, :], -1.0, None, ALU.mult))
        d = dve.chain(lambda e: e.tensor_tensor(etw[:, 1, :], etw[:, 1, :], etw[:, 0, :], ALU.min))
        act.wait(d)
        act.chain(lambda e: e.activation(etw[:, 2, :], etw[:, 1, :], ACT.Exp))
        a = act.do(lambda e: e.activation(etw[:, 3, :], etw[:, 2, :], ACT.Ln, bias=1.0))
        dve.chain(lambda e: e.tensor_scalar(etw[:, 4, :], etw[:, 0, :], 0.0, None, ALU.max))
        dve.wait(a)
        dve.chain(lambda e: e.tensor_tensor(etw[:, 4, :], etw[:, 4, :], etw[:, 3, :], ALU.add))
        have_w8 = dve.chain(lambda e: e.tensor_scalar(etw[:, 5, :], etw[:, 4, :], 8.0, None, ALU.mult))

        for i in range(3):
            last = dve.do(lambda e, i=i: e.tensor_copy(ecol[:, i, :], ecol_i[:, i, :]))
        for s in range(NS):
            last = dve.do(lambda e, s=s: e.memset(ecol[:, 6, s * SUPER:(s + 1) * SUPER], float(16 ** s)))
        dve.wait(last)
        have_key = dve.do(lambda e: e.scalar_tensor_tensor(ecol[:, 3, :], ecol[:, 0, :], float(N), ecol[:, 1, :],
                                                           ALU.mult, ALU.add))
        dve.chain(lambda e: e.tensor_scalar(ecol[:, 4, :], ecol[:, 2, :], 1.0, 1.0, ALU.is_equal, ALU.mult))
        for kind, code in ((2, 2.0), (3, 4.0), (4, 8.0), (0, 8.0)):
            dve.chain(lambda e, kind=kind, code=code: e.tensor_scalar(
                ecol[:, 5, :], ecol[:, 2, :], float(kind), code, ALU.is_equal, ALU.mult))
            dve.chain(lambda e: e.tensor_tensor(ecol[:, 4, :], ecol[:, 4, :], ecol[:, 5, :], ALU.add))
        dve.chain(lambda e: e.tensor_tensor(ecol[:, 4, :], ecol[:, 4, :], ecol[:, 6, :], ALU.mult))

        edge_state = dict(product=None)

        def edge_rows(s):
            if edge_state.get("rows_read"):
                sync.wait(edge_state["rows_read"])
            row_in.load(sync, src_row[:], A["src"][s * SUPER * P:(s + 1) * SUPER * P].partition_broadcast(P))
            got = row_in.load(sync, dst_row[:], A["dst"][s * SUPER * P:(s + 1) * SUPER * P].partition_broadcast(P))
            dve.wait(got, have_later)
            key = dve.chain(lambda e: e.scalar_tensor_tensor(key_row[:], src_row[:], float(N), dst_row[:],
                                                             ALU.mult, ALU.add))
            edge_state["rows_read"] = key
            for j in range(SUPER):
                c, width = s * SUPER + j, (SUPER - j) * P
                last = dve.chain(lambda e, c=c, j=j, width=width: e.scalar_tensor_tensor(
                    same[:, 0:width], key_row[:, j * P:], ecol[:, 3, c:c + 1], later[:, 0:width],
                    ALU.is_equal, ALU.mult, accum_out=ecol[:, 7, c:c + 1]))
            cut = slice(s * SUPER, (s + 1) * SUPER)
            dve.chain(lambda e: e.scalar_tensor_tensor(ecol[:, 4, cut], ecol[:, 7, cut], 0.0, ecol[:, 4, cut],
                                                       ALU.is_equal, ALU.mult))

        def edge_chunk(c):
            o = c % 2
            if c >= 2:
                dve.wait(edge_state[c - 2])
            dve.wait(have_node)
            dve.do(lambda e: e.tensor_scalar(onehot_src[:, o], node[:], ecol[:, 0, c:c + 1], None, ALU.is_equal))
            hot = dve.do(lambda e: e.tensor_scalar(onehot_dst[:, o], node[:], ecol[:, 1, c:c + 1],
                                                   ecol[:, 4, c:c + 1], ALU.is_equal, ALU.mult))
            pe.wait(hot)
            for i in range(NT):
                done = pe.do(lambda e, i=i: e.matmul(bank[i][:, 0:N], onehot_src[:, o, i * P:(i + 1) * P],
                                                     onehot_dst[:, o], start=(c == 0), stop=(c == EC - 1)))
            edge_state[c] = done

        def edge_mask():
            digits = k2[:].rearrange("p k n -> p (k n)")[:, 0:NT * N].rearrange("p (t n) -> p t n", t=NT)
            kind = k2[:].rearrange("p k n -> p (k n)")[:, NT * N:2 * NT * N].rearrange("p (t n) -> p t n", t=NT)
            dve.wait(edge_state[EC - 1], have_diag, have_w8)
            for i in range(NT):
                last = bank_read[i] = dve.do(lambda e, i=i: e.tensor_tensor(digits[:, i], bank[i][:, 0:N],
                                                                            diag[:, i], ALU.max))
            dve.wait(last)
            dve.do(lambda e: e.tensor_scalar(mask8[:], digits, 0.0, 8.0 * ABSENT, ALU.is_equal, ALU.mult))
            dve.chain(lambda e: e.tensor_scalar(kind.bitcast(I32), digits.bitcast(I32), 23, 3,
                                                ALU.logical_shift_right, ALU.bitwise_and))
            for w, code in enumerate((3.0, 0.0, 1.0, 2.0)):
                dve.chain(lambda e, w=w, code=code: e.tensor_scalar(
                    digits, kind.bitcast(I32), code, etw[:, 5, w:w + 1], ALU.is_equal, ALU.mult))
                last = dve.chain(lambda e: e.tensor_tensor(mask8[:], mask8[:], digits, ALU.add))
            return last

        normed = layer_norm(rows, got_small)
        transpose_rows(rows, normed, (3, 4, 5, 6, 7))

        x_in, mid = (in_hi, in_lo), (mid_hi, mid_lo)

        def to_mid(col):
            return lambda k, bk, done: split_out(bk, N, mid_hi[:, k, :], mid_lo[:, k, :], done,
                                                 bias=cols[:, col, k:k + 1])

        def to_plain(target, col):
            def evacuate(k, bk, done):
                act.wait(done)
                return act.do(lambda e: e.activation(target[:, k, :], bank[bk][:, 0:N], ACT.Identity,
                                                     bias=cols[:, col, k:k + 1]))
            return evacuate

        edge_work = []
        for s in range(NS):
            edge_work.append(lambda s=s: edge_rows(s))
            edge_work += [lambda c=c: edge_chunk(c) for c in range(s * SUPER, (s + 1) * SUPER)]

        def between():
            for _ in range(3):
                if edge_work:
                    edge_work.pop(0)()

        act.wait(got_small)
        evacuations = [(x_in, to_mid(0)), (mid, to_plain(q2, 1)), (x_in, to_mid(2)), (mid, to_plain(k2, 3)),
                       (x_in, to_mid(4))]
        have_mask = None
        for n, (source, evacuate) in enumerate(evacuations):
            if n == 3:
                while edge_work:
                    edge_work.pop(0)()
                have_mask = edge_mask()
                act.wait(have_mask)
            for c in range(2):
                for _ in product_cols(source, c, evacuate):
                    between()

        def to_v2(c):
            def evacuate(i, bk, done):
                dve.wait(done, biv_in)
                return dve.do(lambda e: e.tensor_tensor(v2[:, i, c * HALF:(c + 1) * HALF], bank[bk][:],
                                                        row_bias[:, c * HALF:(c + 1) * HALF], ALU.add))
            return evacuate

        for c in range(2):
            product_rows(mid, to_v2(c), (0, 1, 2) if c else (3, 4, 5))
        have_v2 = bank_read[2]
        sync.wait(have_v2)
        bo_in = bias_in.load(sync, row_bias[:], A["bo"].partition_broadcast(P))

        pe.wait((act.sem, act.count), have_v2)
        units = [(h, i) for h in range(HEADS) for i in range(NT)]
        token = {}

        def scores(n):
            h, i = units[n]
            base, k = (h % 2) * DH, h // 2
            bk = n % 3
            if bank_read[bk]:
                pe.wait(bank_read[bk])
            token["s", n] = pe.do(lambda e: e.matmul(bank[bk][:, 0:N], q2[base:base + DH, k, i * P:(i + 1) * P],
                                                     k2[base:base + DH, k, :], start=True, stop=True))

        def softmax(n):
            bk, o, q, pb = n % 3, n % 2, n % 4, n % 3
            if n >= 2:
                dve.wait(token["e", n - 2])
            dve.wait(token["s", n], have_mask)
            m = bank_read[bk] = dve.do(lambda e: e.tensor_tensor_reduce(
                out=score[:, o], in0=bank[bk][:, 0:N], in1=mask8[:, units[n][1]],
                scale=-1.0 / 8.0, scalar=3.0e38, op0=ALU.add, op1=ALU.min, accum_out=sums[:, q, 0:1]))
            act.wait(m)
            if n >= 3:
                act.wait(token["t", n - 3])
            token["e", n] = act.do(lambda e: e.activation(prob[:, pb], score[:, o], ACT.Exp, scale=-1.0,
                                                          bias=sums[:, q, 0:1], accum_out=sums[:, q, 1:2]))
            dve.wait(token["e", n])
            dve.chain(lambda e: e.reciprocal(sums[:, q, 1:2], sums[:, q, 1:2]))
            token["p", n] = dve.do(lambda e: e.tensor_scalar(prob[:, pb], prob[:, pb], sums[:, q, 1:2], None, ALU.mult))

        def turn_probabilities(n):
            h, i = units[n]
            bk, o = 3 + n % 2, n % 3
            if bank_read[bk]:
                pe.wait(bank_read[bk])
            pe.wait(token["p", n])
            for m in range(NT):
                done = pe.do(lambda e, m=m: e.transpose(bank[bk][:, m * P:(m + 1) * P],
                                                        prob[:, o, m * P:(m + 1) * P], ident[:]))
            token["t", n] = done
            act.wait(done)
            if h >= 2:
                act.wait(token["o", h - 2])
            for m in range(1):
                bank_read[bk] = token["c", n] = act.do(lambda e: e.activation(
                    prob_t[:, h % 2, :, i * P:(i + 1) * P],
                    bank[bk][:, 0:N].rearrange("p (m n) -> p m n", m=NT), ACT.Copy))

        def attend(h):
            bk = 5 + (h // 2) % 2
            base = (h % 2) * DH
            if h % 2 == 0 and bank_read[bk]:
                pe.wait(bank_read[bk])
            pe.wait(token["c", NT * h + NT - 1])
            for m in range(NT):
                done = pe.do(lambda e, m=m: e.matmul(bank[bk][base:base + DH, 0:N], v2[:, m, h * DH:(h + 1) * DH],
                                                     prob_t[:, h % 2, m, :], start=(m == 0), stop=(m == NT - 1)))
            token["o", h] = done
            if h % 2:
                bank_read[bk] = split_out(bk, N, in_hi[:, h // 2, :], in_lo[:, h // 2, :], done)

        AHEAD = 2
        for n in range(len(units) + AHEAD + 1):
            if n < len(units):
                scores(n)
            if n >= AHEAD and n - AHEAD < len(units):
                turn_probabilities(n - AHEAD)
                if units[n - AHEAD][1] == NT - 1 and units[n - AHEAD][0] > 0:
                    attend(units[n - AHEAD][0] - 1)
            if n < len(units):
                softmax(n)
        attend(HEADS - 1)

        def to_residual(c):
            cut = slice(c * HALF, (c + 1) * HALF)

            def evacuate(i, bk, done):
                dve.wait(done, bo_in)
                got = dve.do(lambda e: e.tensor_tensor(v2[:, i, cut], bank[bk][:], row_bias[:, cut], ALU.add))
                dve.wait(got)
                token["x", i, c] = dve.do(lambda e: e.tensor_tensor(x_rows[:, i, cut], x_rows[:, i, cut],
                                                                   v2[:, i, cut], ALU.add))
                return got
            return evacuate

        pe.wait(bank_read[5], bank_read[6])
        for c in range(2):
            product_rows(x_in, to_residual(c), (0, 1, 2) if c else (3, 4, 7))

        normed = layer_norm(rows2, token["x", NT - 1, 1])
        sync.wait(token["x", NT - 1, 1])
        small.load(sync, router_raw[:], A["router"].rearrange("(k p) e -> p k e", p=P))
        got_router = small.load(sync, e_bias[:], A["e_bias"].partition_broadcast(P))
        act.wait(got_router)
        dve.wait(got_router)
        hi = act.do(lambda e: e.activation(router_hi[:], router_raw[:], ACT.Copy))
        dve.wait(hi)
        have_router = dve.do(lambda e: e.tensor_tensor(router_lo[:], router_raw[:], router_hi[:].bitcast(F32),
                                                       ALU.subtract))
        turned = transpose_rows(rows2, normed, (6, 7))
        pool.wait(token["x", NT - 1, 1])
        pool.chain(lambda e: e.memset(earlier[:], 1.0))
        have_earlier = pool.do(lambda e: e.affine_select(
            out=earlier[:], in_=earlier[:], compare_op=ALU.is_gt, fill=0.0, base=0,
            pattern=[[1, EXPERTS], [-1, EXPERTS]], channel_multiplier=0))

        pe.wait(turned, have_router, bank_read[0])
        for i in range(NT):
            for k in range(KT):
                for m, (a, w) in enumerate(PASSES):
                    done = pe.do(lambda e, i=i, k=k, m=m, a=a, w=w: e.matmul(
                        bank[0][:, i * EXPERTS:(i + 1) * EXPERTS], x_in[a][:, k, i * P:(i + 1) * P],
                        (router_hi, router_lo)[w][:, k, :], start=(k == 0 and m == 0),
                        stop=(k == KT - 1 and m == 2)))
        act.wait(done)
        bank_read[0] = sig = act.do(lambda e: e.activation(
            prob_e[:], bank[0][:, 0:NT * EXPERTS].rearrange("p (t e) -> p t e", t=NT), ACT.Sigmoid))

        def route():
            dve.wait(sig, got_router, have_earlier)
            s_, masked, chosen, tmp = r
            for i in range(NT):
                last = dve.do(lambda e, i=i: e.tensor_tensor(s_[:, i], prob_e[:, i], e_bias[:], ALU.add))
            dve.wait(last)
            four = s_[:].rearrange("p t (g s) -> p t g s", s=GSIZE)
            a_, b_, c_, d_ = (four[:, :, :, j] for j in range(GSIZE))
            dve.do(lambda e: e.tensor_tensor(gs[:, :, 0], a_, b_, ALU.max))
            dve.do(lambda e: e.tensor_tensor(gs[:, :, 1], a_, b_, ALU.min))
            dve.do(lambda e: e.tensor_tensor(gs[:, :, 2], c_, d_, ALU.max))
            dve.chain(lambda e: e.tensor_tensor(gs[:, :, 3], c_, d_, ALU.min))
            dve.do(lambda e: e.tensor_tensor(gs[:, :, 4], gs[:, :, 0], gs[:, :, 2], ALU.max))
            dve.do(lambda e: e.tensor_tensor(gs[:, :, 5], gs[:, :, 0], gs[:, :, 2], ALU.min))
            dve.chain(lambda e: e.tensor_tensor(gs[:, :, 1], gs[:, :, 1], gs[:, :, 3], ALU.max))
            dve.chain(lambda e: e.tensor_tensor(gs[:, :, 5], gs[:, :, 5], gs[:, :, 1], ALU.max))
            dve.chain(lambda e: e.tensor_tensor(gs[:, :, 0], gs[:, :, 4], gs[:, :, 5], ALU.add))

            def rank_of(values, n, result):
                rival = values.unsqueeze(1).to_broadcast([P, n, n])
                own = values.unsqueeze(2).to_broadcast([P, n, n])
                bb, b2 = beats[:, 0:n, 0:n], beats2[:, 0:n, 0:n]
                dve.do(lambda e: e.tensor_tensor(bb, rival, own, ALU.is_gt))
                dve.chain(lambda e: e.tensor_tensor(b2, rival, own, ALU.is_equal))
                dve.chain(lambda e: e.tensor_tensor(b2, b2, earlier[:, 0:n, 0:n], ALU.mult))
                dve.chain(lambda e: e.tensor_tensor(bb, bb, b2, ALU.add))
                dve.chain(lambda e: e.tensor_reduce(result, bb, AX.X, ALU.add))

            for i in range(NT):
                rank_of(gs[:, i, 0], GROUPS, gs[:, i, 1])
            dve.chain(lambda e: e.tensor_scalar(gs[:, :, 2], gs[:, :, 1], 1.5, None, ALU.is_lt))
            dve.chain(lambda e: e.tensor_scalar(gs[:, :, 3], gs[:, :, 2], -1.0, None, ALU.add))
            for i in range(NT):
                inside = gs[:, i, 2].unsqueeze(2).to_broadcast([P, GROUPS, GSIZE])
                less = gs[:, i, 3].unsqueeze(2).to_broadcast([P, GROUPS, GSIZE])
                dve.chain(lambda e, i=i, inside=inside: e.tensor_tensor(
                    masked[:, i].rearrange("p (g s) -> p g s", s=GSIZE), four[:, i], inside, ALU.mult))
                dve.chain(lambda e, i=i, less=less: e.tensor_tensor(
                    masked[:, i].rearrange("p (g s) -> p g s", s=GSIZE),
                    masked[:, i].rearrange("p (g s) -> p g s", s=GSIZE), less, ALU.add))
            for i in range(NT):
                rank_of(masked[:, i], EXPERTS, tmp[:, i])
            dve.chain(lambda e: e.tensor_scalar(chosen[:], tmp[:], GSIZE - 0.5, None, ALU.is_lt))
            dve.chain(lambda e: e.tensor_tensor(tmp[:], chosen[:], prob_e[:], ALU.mult))
            dve.chain(lambda e: e.tensor_reduce(denom[:], tmp[:], AX.X, ALU.add))
            dve.chain(lambda e: e.tensor_scalar(denom[:], denom[:], 1e-20, None, ALU.add))
            dve.chain(lambda e: e.reciprocal(denom[:], denom[:]))
            for i in range(NT):
                last = dve.do(lambda e, i=i: e.tensor_scalar(combine[:, i], tmp[:, i], denom[:, i:i + 1],
                                                             ROUTE_SCALE, ALU.mult, ALU.mult))
            dve.wait(last)

        deferred = []
        state = dict(hidden=0)
        hidden_read = [None, None]

        def unit(u):
            weight = None if u < SHARED else u - SHARED
            for c in range(2):
                silu = {}

                def gate_out(i, bk, done):
                    act.wait(done)
                    if ("h", i) in token:
                        act.wait(token["h", i])
                    silu[i] = act.do(lambda e: e.activation(gated[:, i], bank[bk][:], ACT.Silu))
                    return silu[i]

                def up_out(i, bk, done, c=c):
                    o = state["hidden"] % 2
                    state["hidden"] += 1
                    dve.wait(done, silu[i])
                    if hidden_read[o]:
                        dve.wait(hidden_read[o])
                    h = token["h", i] = dve.do(lambda e: e.tensor_tensor(hidden[:, o], bank[bk][:], gated[:, i],
                                                                        ALU.mult))
                    tb = 6 + o
                    pe_work = lambda: turn_hidden(c, i, o, tb, h)
                    if len(deferred) >= 1:
                        deferred.pop(0)()
                    deferred.append(pe_work)
                    return h

                product_rows(x_in, gate_out, (0, 1, 2), behind=tuple(deferred))
                deferred.clear()
                product_rows(x_in, up_out, (3, 4, 5))
            def down_out(c):
                def evacuate(i, bk, done):
                    cut = slice(c * HALF, (c + 1) * HALF)
                    dve.wait(done)
                    if weight is None:
                        return dve.do(lambda e: e.tensor_tensor(x_rows[:, i, cut], bank[bk][:], x_rows[:, i, cut],
                                                                ALU.add))
                    return dve.do(lambda e: e.scalar_tensor_tensor(
                        x_rows[:, i, cut], bank[bk][:], combine[:, i, weight:weight + 1], x_rows[:, i, cut],
                        ALU.mult, ALU.add))
                return evacuate
            while deferred:
                deferred.pop(0)()
            dve.wait((dve.sem, dve.count))
            pe.wait((dve.sem, dve.count))
            product_rows((act_hi, act_lo), down_out(0), (0, 1, 2))
            product_rows((act_hi, act_lo), down_out(1), (3, 4, 5))

        def turn_hidden(c, i, o, tb, ready):
            pe.wait(ready)
            if bank_read[tb]:
                pe.wait(bank_read[tb])
            for m in range(HALF // P):
                done = pe.do(lambda e, m=m: e.transpose(bank[tb][:, m * P:(m + 1) * P],
                                                        hidden[:, o, m * P:(m + 1) * P], ident[:]))
            hidden_read[o] = done
            ks = slice(c * (HALF // P), (c + 1) * (HALF // P))
            hi, lo = act_hi[:, ks, i * P:(i + 1) * P], act_lo[:, ks, i * P:(i + 1) * P]
            four = bank[tb][:].rearrange("p (k n) -> p k n", n=P)
            act.wait(done)
            h = act.do(lambda e: e.activation(hi, four, ACT.Copy))
            dve.wait(h)
            bank_read[tb] = dve.do(lambda e: e.tensor_tensor(lo, four, hi.bitcast(F32), ALU.subtract))

        unit(0)
        route()
        for u in range(1, UNITS):
            unit(u)
        assert taken[0] == len(pieces)

        sync.wait((dve.sem, dve.count))
        out_done = Arrival(sem("out_done"))
        written = out_done.load(sync, out.rearrange("(t p) d -> p t d", p=P), x_rows[:])
        sync.wait(written)

        block = ctx.enter_context(nc.Block())
        block.sync(sync.emit)
        block.gpsimd(pool.emit)
        block.scalar(act.emit)
        block.vector(dve.emit)
        block.tensor(pe.emit)


def kernel(**inputs):
    import concourse.bacc as bacc
    from concourse.bass_utils import run_bass_kernel_spmd

    def get(name):
        return np.ascontiguousarray(inputs[name])

    def columns(v):
        return np.ascontiguousarray(v.reshape(-1, P).T)

    arrays = {"x": get("x"), "src": get("src"), "dst": get("dst"),
              "src_cols": columns(get("src")), "dst_cols": columns(get("dst")),
              "type_cols": columns(get("edge_type_5")), "etw": get("L0_gnn_edge_type_weights")}
    for name in ("wq", "wk", "wv", "wiq", "wik", "wiv", "wo"):
        arrays[name] = np.ascontiguousarray(get("L0_gnn_" + name).T)
    for name in ("bq", "bk", "bv", "biq", "bik"):
        arrays[name] = columns(get("L0_gnn_" + name))
    arrays.update(biv=get("L0_gnn_biv"), bo=get("L0_gnn_bo"),
                  router=np.ascontiguousarray(get("L0_ffn_router_w").T), e_bias=get("L0_ffn_bias"),
                  gate=get("L0_ffn_gate_w"), up=get("L0_ffn_up_w"), down=get("L0_ffn_down_w"),
                  sh_gate=get("L0_ffn_sh_gate_w"), sh_up=get("L0_ffn_sh_up_w"),
                  sh_down=get("L0_ffn_sh_down_w"))

    nc = bacc.Bacc("TRN2", target_bir_lowering=False, num_devices=1)
    aps = {name: nc.dram_tensor("in_" + name, a.shape, mybir.dt.from_np(a.dtype), kind="ExternalInput").ap()
           for name, a in arrays.items()}
    out = nc.dram_tensor("result", (N, D), F32, kind="ExternalOutput").ap()
    build(nc, aps, out)
    ran = run_bass_kernel_spmd(nc, [{"in_" + name: a for name, a in arrays.items()}], core_ids=[0])
    return ran.results[0]["result"]
```

```python
from contextlib import ExitStack, contextmanager

import numpy as np
import concourse.bass as bass
from concourse import mybir
from concourse.alu_op_type import AluOpType as ALU

F32 = mybir.dt.float32
F32R = mybir.dt.float32r
BF16 = mybir.dt.bfloat16
I32 = mybir.dt.int32
ACT = mybir.ActivationFunctionType
AX = mybir.AxisListType

P = 128
N = 384
NT = N // P
D = 1024
KT = D // P
HEADS = 16
DH = D // HEADS
EDGES = 6144
EC = EDGES // P
SUPER = 8
NS = EC // SUPER
EXPERTS = 16
GROUPS = 4
GSIZE = EXPERTS // GROUPS
SHARED = 2
ROUTE_SCALE = 2.5
EPS = 1e-5
ABSENT = -1.0e30

HALF = 512
KPIECE = 4
RAW = 4
SPLIT = 4


class Lane:

    def __init__(self, sems):
        self.sems, self.track = sems, 0
        self.counts, self.steps, self.waited = [0] * len(sems), [], {}

    def wait(self, *tokens):
        for sem, value in tokens:
            if self.waited.get(id(sem), 0) < value:
                self.waited[id(sem)] = value
                self.steps.append(lambda e, s=sem, v=value: e.wait_ge(s, v))

    def run(self, step):
        self.steps.append(step)

    def do(self, step):
        sem = self.sems[self.track]
        self.counts[self.track] += 1
        self.steps.append(lambda e: step(e).then_inc(sem, 1))
        return sem, self.counts[self.track]

    def chain(self, step):
        done = self.do(step)
        self.wait(done)
        return done

    def emit(self, engine):
        for step in self.steps:
            step(engine)


class Arrival:

    def __init__(self, sem):
        self.sem, self.count = sem, 0

    def load(self, lane, out, in_):
        return self.start(lane, lambda e: e.dma_start(out, in_))

    def start(self, lane, step):
        self.count += 16
        lane.run(lambda e: step(e).then_inc(self.sem, 16))
        return self.sem, self.count


class Operand:

    def __init__(self, hi, lo):
        self.hi, self.lo, self.ready = hi, lo, {}

    def when(self, k, i):
        return [self.ready[x] for x in (k, (k, i)) if x in self.ready]


def build(nc, A, normed_dram, out):
    with ExitStack() as ctx, ExitStack() as gnn_buffers:
        def sb(name, shape, dt=F32, scope=ctx):
            return scope.enter_context(nc.sbuf_tensor(name, shape, dt))

        def sem(name):
            return ctx.enter_context(nc.semaphore(name))

        bank = [ctx.enter_context(nc.psum_tensor(f"bank{i}", [P, HALF], F32)) for i in range(8)]
        bank_read = [{} for _ in range(8)]

        raw = sb("raw", [P, RAW, KPIECE, HALF])
        w_hi = sb("w_hi", [P, SPLIT, KPIECE, HALF], F32R)
        w_lo = sb("w_lo", [P, SPLIT, KPIECE, HALF], F32R)
        in_hi = sb("in_hi", [P, KT, N], F32R)
        in_lo = sb("in_lo", [P, KT, N], F32R)
        x_rows = sb("x_rows", [P, NT, D])
        ident = sb("ident", [P, P])
        stats = sb("stats", [P, NT, 2, 6])
        meanvar = sb("meanvar", [P, NT, 2])
        rstd = sb("rstd", [P, NT])
        half_neg = sb("half_neg", [P, NT])
        cols = sb("cols", [P, 5, KT])

        g = gnn_buffers
        mid_hi = sb("mid_hi", [P, KT, N], F32R, g)
        mid_lo = sb("mid_lo", [P, KT, N], F32R, g)
        q2 = sb("q2", [P, KT, N], F32, g)
        rows = q2[:].rearrange("p k n -> p (k n)").rearrange("p (t d) -> p t d", t=NT)
        k2 = sb("k2", [P, KT, N], F32, g)
        k2_flat = k2[:].rearrange("p k n -> p (k n)")
        x_again = k2_flat.rearrange("p (t d) -> p t d", t=NT)
        v2 = x_rows
        mask8 = sb("mask8", [P, NT, N], F32, g)
        sums = sb("sums", [P, 4, 2], F32, g)
        etw = sb("etw", [P, 6, 4], F32, g)
        with ExitStack() as edge_buffers:
            b = edge_buffers
            src_row = k2_flat[:, 0:SUPER * P].bitcast(I32)
            dst_row = k2_flat[:, SUPER * P:2 * SUPER * P].bitcast(I32)
            key_row = k2_flat[:, 2 * SUPER * P:3 * SUPER * P]
            later = sb("later", [P, SUPER * P], BF16, b)
            same = sb("same", [P, SUPER * P], BF16, b)
            onehot_src = sb("onehot_src", [P, 2, N], BF16, b)
            onehot_dst = sb("onehot_dst", [P, 2, N], BF16, b)
            node = sb("node", [P, N], F32, b)
            diag = sb("diag", [P, NT, N], F32, b)
            ecol_i = sb("ecol_i", [P, 3, EC], I32, b)
            ecol = sb("ecol", [P, 8, EC], F32, b)
        with ExitStack() as attention_buffers:
            b = attention_buffers
            score = sb("score", [P, 2, N], F32, b)
            prob = sb("prob", [P, 3, N], F32, b)
            prob_t = sb("prob_t", [P, 2, NT, N], F32, b)
            row_bias = prob_t[:].rearrange("p a m n -> p (a m n)")[:, 0:D]
        gnn_buffers.close()

        act_hi = sb("act_hi", [P, KT, N], F32R)
        act_lo = sb("act_lo", [P, KT, N], F32R)
        rows2 = sb("rows2", [P, NT, D])
        gated = sb("gated", [P, NT, HALF])
        hidden = sb("hidden", [P, NT, HALF])
        router_raw = sb("router_raw", [P, KT, EXPERTS])
        router_hi = sb("router_hi", [P, KT, EXPERTS], F32R)
        router_lo = sb("router_lo", [P, KT, EXPERTS], F32R)
        e_bias = sb("e_bias", [P, EXPERTS])
        prob_e = sb("prob_e", [P, NT, EXPERTS])
        r = [sb(f"route{i}", [P, NT, EXPERTS]) for i in range(4)]
        gs = sb("gs", [P, NT, 6, GROUPS])
        beats = sb("beats", [P, EXPERTS, EXPERTS])
        beats2 = sb("beats2", [P, EXPERTS, EXPERTS])
        earlier = sb("earlier", [P, EXPERTS, EXPERTS])
        combine = sb("combine", [P, NT, EXPERTS])
        denom = sb("denom", [P, NT])
        chosen16 = sb("chosen16", [P, NT, EXPERTS], BF16)
        before = sb("before", [P, P], BF16)
        ones16 = sb("ones16", [P, P], BF16)
        place = sb("place", [P, NT + 1, EXPERTS])
        slot = sb("slot", [P, N])
        token_id = sb("token_id", [P, NT])
        info = sb("info", [P, NT, EXPERTS, 4], F32R)
        chooses = sb("chooses", [P, NT, N], F32R)
        slots = sb("slots", [P, EXPERTS * NT, 4])
        spare_row = sb("spare_row", [P, 2])
        slot_w = sb("slot_w", [P, EXPERTS * NT])
        slot_to = sb("slot_to", [P, EXPERTS * NT])
        gather_at = sb("gather_at", [P, EXPERTS * NT], I32)
        scatter_at = sb("scatter_at", [P, EXPERTS * NT], I32)
        counts = sb("counts", [P, EXPERTS], I32)
        idle = sb("idle", [1, 2 * NT])

        pe, act, dve, pool = (Lane([sem(f"{n}_done{t or ''}") for t in range(NT)])
                              for n in ("tensor", "scalar", "vector", "gpsimd"))
        sync = Lane([None])
        raw_in = [Arrival(sem(f"raw_in{i}")) for i in range(RAW)]

        def read_by(bk, *tokens):
            if pe.track == 0:
                bank_read[bk] = {}
            for s_, v in tokens:
                bank_read[bk][id(s_)] = (s_, v)

        def wait_bank(bk):
            pe.wait(*bank_read[bk].values())

        pieces = []
        raw_free = [None] * RAW
        split_free = [[]] * SPLIT

        def piece(w, c, kh):
            return w.rearrange("(k p) f -> p k f", p=P)[:, kh * KPIECE:(kh + 1) * KPIECE,
                                                        c * HALF:(c + 1) * HALF]

        for w in ("wq", "wiq", "wk", "wik", "wv", "wiv", "wo"):
            pieces += [piece(A[w], c, kh) for c in range(2) for kh in range(2)]

        def unit_matrices(u):
            if u < SHARED:
                cut = slice(u * D, (u + 1) * D)
                return A["sh_gate"][:, cut], A["sh_up"][:, cut], A["sh_down"][cut, :]
            return A["gate"][u - SHARED], A["up"][u - SHARED], A["down"][u - SHARED]

        UNITS = SHARED + EXPERTS
        for u in range(UNITS):
            gate, up, down = unit_matrices(u)
            for c in range(2):
                pieces += [piece(w, c, kh) for w in (gate, up) for kh in range(2)]
            pieces += [piece(down, c, kh) for kh in range(2) for c in range(2)]

        loaded, splits, taken = [], [], [0]

        def load_ahead(upto):
            while len(loaded) < min(upto, len(pieces)):
                i = len(loaded)
                s = i % RAW
                if raw_free[s]:
                    sync.wait(raw_free[s])
                loaded.append(raw_in[s].load(sync, raw[:, s], pieces[i]))

        def split_ahead(upto):
            while len(splits) < min(upto, len(pieces)):
                i = len(splits)
                load_ahead(i + 1)
                s, t = i % RAW, i % SPLIT
                act.wait(loaded[i], *split_free[t])
                hi = act.do(lambda e, s=s, t=t: e.activation(w_hi[:, t], raw[:, s], ACT.Copy))
                dve.wait(hi)
                lo = dve.do(lambda e, s=s, t=t: e.tensor_tensor(
                    w_lo[:, t], raw[:, s], w_hi[:, t].bitcast(F32), ALU.subtract))
                raw_free[s] = lo
                splits.append((hi, lo))
                load_ahead(i + 1 + RAW)

        def next_piece(ahead):
            i = taken[0]
            taken[0] += 1
            split_ahead(i + ahead)
            return i % SPLIT, splits[i]

        PASSES = ((0, 0), (1, 0), (0, 1))

        def rows_piece(operand, i, t, kh, bk):
            if kh == 0:
                wait_bank(bk)
            for n in range(KPIECE):
                k = kh * KPIECE + n
                pe.wait(*operand.when(k, i))
                for m, (a, w) in enumerate(PASSES):
                    first, last = k == 0 and m == 0, k == KT - 1 and m == 2
                    step = (lambda e, k=k, a=a, w=w, n=n, first=first, last=last:
                            e.matmul(bank[bk][:], (operand.hi, operand.lo)[a][:, k, i * P:(i + 1) * P],
                                     (w_hi, w_lo)[w][:, t, n], start=first, stop=last))
                    if n == KPIECE - 1 and m == 2:
                        return pe.do(step)
                    pe.run(step)

        def product_rows(operand, evacuate, banks):
            for kh in range(2):
                t, ready = next_piece(SPLIT)
                pe.wait(*ready)
                for i in range(NT):
                    done = rows_piece(operand, i, t, kh, banks[i])
                    if kh == 1:
                        read_by(banks[i], evacuate(i, banks[i], done))
                split_free[t] = [done]

        turn = [0]

        def product_cols(operand, c, evacuate):
            ring = (3, 4, 5, 6, 7)
            banks = [ring[(turn[0] + m) % 5] for m in range(4)]
            turn[0] += 4
            for kh in range(2):
                t, ready = next_piece(SPLIT)
                pe.wait(*ready)
                for f in range(HALF // P):
                    bk = banks[f]
                    if kh == 0:
                        wait_bank(bk)
                    for n in range(KPIECE):
                        k = kh * KPIECE + n
                        pe.wait(*operand.when(k, 0))
                        for m, (a, w) in enumerate(PASSES):
                            first, last = k == 0 and m == 0, k == KT - 1 and m == 2
                            step = (lambda e, bk=bk, k=k, f=f, a=a, w=w, n=n, t=t, first=first, last=last:
                                    e.matmul(bank[bk][:, 0:N], (w_hi, w_lo)[w][:, t, n, f * P:(f + 1) * P],
                                             (operand.hi, operand.lo)[a][:, k, :], start=first, stop=last))
                            if n == KPIECE - 1 and m == 2:
                                done = pe.do(step)
                            else:
                                pe.run(step)
                    if kh == 1:
                        read_by(bk, evacuate(c * (HALF // P) + f, bk, done))
                split_free[t] = [done]
                yield

        x_in_sem = Arrival(sem("x_in"))
        got_x = x_in_sem.load(sync, x_rows[:], A["x"].rearrange("(t p) d -> p t d", p=P))
        load_ahead(RAW)
        small = Arrival(sem("small_in"))
        for i, name in enumerate(("bq", "biq", "bk", "bik", "bv")):
            small.load(act, cols[:, i, :], A[name])
        for i, name in enumerate(("src_cols", "dst_cols", "type_cols")):
            small.load(act, ecol_i[:, i, :], A[name])
        got_small = small.load(act, etw[:, 0, :], A["etw"].partition_broadcast(P))

        row_in = Arrival(sem("edge_rows_in"))
        bias_in = Arrival(sem("bias_in"))

        pool.do(lambda e: e.memset(ident[:], 0.0))
        have_half = pool.do(lambda e: e.memset(half_neg[:], -0.5))
        pool.chain(lambda e: e.memset(diag[:], 0.0))
        have_ident = pool.do(lambda e: e.affine_select(out=ident[:], in_=ident[:], compare_op=ALU.not_equal,
                                                       fill=1.0, base=0, pattern=[[-1, P]],
                                                       channel_multiplier=1))
        have_diag = pool.do(lambda e: e.affine_select(out=diag[:], in_=diag[:], compare_op=ALU.not_equal,
                                                      fill=0.5, base=0, pattern=[[P, NT], [-1, N]],
                                                      channel_multiplier=1))
        have_node = pool.do(lambda e: e.iota(node[:], pattern=[[1, N]], base=0, channel_multiplier=0,
                                             allow_small_or_imprecise_dtypes=True))
        pool.chain(lambda e: e.memset(later[:], 1.0))
        have_later = pool.do(lambda e: e.affine_select(out=later[:], in_=later[:], compare_op=ALU.is_gt,
                                                       fill=0.0, base=0, pattern=[[1, SUPER * P]],
                                                       channel_multiplier=-1))

        def layer_norm(target, ready):
            for i in range(NT):
                for hh in range(2):
                    dve.wait(*ready(i, hh))
                    stat = dve.do(lambda e, i=i, hh=hh: e.bn_stats(stats[:, i, hh, :],
                                                                   x_rows[:, i, hh * HALF:(hh + 1) * HALF]))
            dve.wait(stat)
            for i in range(NT):
                agg = dve.do(lambda e, i=i: e.bn_aggr(meanvar[:, i, :],
                                                      stats[:, i].rearrange("p a b -> p (a b)")))
            dve.wait(agg)
            var = dve.do(lambda e: e.tensor_scalar(rstd[:], meanvar[:, :, 1], EPS, None, ALU.add))
            pool.wait(var, have_half)
            power = pool.do(lambda e: e.tensor_tensor(rstd[:], rstd[:], half_neg[:], ALU.pow))
            dve.wait(power)
            done = []
            for i in range(NT):
                done.append(dve.do(lambda e, i=i: e.tensor_scalar(target[:, i, :], x_rows[:, i, :],
                                                                  meanvar[:, i, 0:1], rstd[:, i:i + 1],
                                                                  ALU.subtract, ALU.mult)))
            return done

        def split_out(bk, source, hi, lo, ready, bias=None):
            act.wait(ready)
            if bias is None:
                h = act.do(lambda e: e.activation(hi, source, ACT.Copy))
                dve.wait(h)
                done = dve.do(lambda e: e.tensor_tensor(lo, source, hi.bitcast(F32), ALU.subtract))
            else:
                h = act.do(lambda e: e.activation(hi, source, ACT.Identity, bias=bias))
                dve.wait(h)
                done = dve.do(lambda e: e.scalar_tensor_tensor(lo, source, bias, hi.bitcast(F32),
                                                               ALU.add, ALU.subtract))
            read_by(bk, done)
            return done

        def transpose_rows(source, ready, banks, target):
            pe.wait(have_ident, *ready)
            for k in range(KT):
                bk = banks[k % len(banks)]
                wait_bank(bk)
                for i in range(NT):
                    step = (lambda e, i=i, k=k, bk=bk: e.transpose(
                        bank[bk][:, i * P:(i + 1) * P], source[:, i, k * P:(k + 1) * P], ident[:]))
                    done = pe.do(step)
                target.ready[k] = split_out(bk, bank[bk][:, 0:N], target.hi[:, k, :], target.lo[:, k, :], done)

        def edge_weights():
            dve.wait(got_small)
            act.wait(got_small)
            dve.chain(lambda e: e.tensor_scalar(etw[:, 1, :], etw[:, 0, :], -1.0, None, ALU.mult))
            d = dve.chain(lambda e: e.tensor_tensor(etw[:, 1, :], etw[:, 1, :], etw[:, 0, :], ALU.min))
            act.wait(d)
            act.chain(lambda e: e.activation(etw[:, 2, :], etw[:, 1, :], ACT.Exp))
            a = act.do(lambda e: e.activation(etw[:, 3, :], etw[:, 2, :], ACT.Ln, bias=1.0))
            dve.chain(lambda e: e.tensor_scalar(etw[:, 4, :], etw[:, 0, :], 0.0, None, ALU.max))
            dve.wait(a)
            dve.chain(lambda e: e.tensor_tensor(etw[:, 4, :], etw[:, 4, :], etw[:, 3, :], ALU.add))
            dve.chain(lambda e: e.tensor_scalar(etw[:, 5, :], etw[:, 4, :], 8.0, None, ALU.mult))

        def edge_values():
            for i in range(3):
                last = dve.do(lambda e, i=i: e.tensor_copy(ecol[:, i, :], ecol_i[:, i, :]))
            for s in range(NS):
                last = dve.do(lambda e, s=s: e.memset(ecol[:, 6, s * SUPER:(s + 1) * SUPER], float(16 ** s)))
            dve.wait(last)
            dve.do(lambda e: e.scalar_tensor_tensor(ecol[:, 3, :], ecol[:, 0, :], float(N), ecol[:, 1, :],
                                                    ALU.mult, ALU.add))
            dve.chain(lambda e: e.tensor_scalar(ecol[:, 4, :], ecol[:, 2, :], 1.0, 1.0, ALU.is_equal, ALU.mult))
            for kind, code in ((2, 2.0), (3, 4.0), (4, 8.0), (0, 8.0)):
                dve.chain(lambda e, kind=kind, code=code: e.tensor_scalar(
                    ecol[:, 5, :], ecol[:, 2, :], float(kind), code, ALU.is_equal, ALU.mult))
                dve.chain(lambda e: e.tensor_tensor(ecol[:, 4, :], ecol[:, 4, :], ecol[:, 5, :], ALU.add))
            dve.chain(lambda e: e.tensor_tensor(ecol[:, 4, :], ecol[:, 4, :], ecol[:, 6, :], ALU.mult))

        edge_state = {}

        def load_edge_rows(s):
            if "rows_read" in edge_state:
                pool.wait(edge_state["rows_read"])
            row_in.load(pool, src_row, A["src"][s * SUPER * P:(s + 1) * SUPER * P].partition_broadcast(P))
            edge_state["rows"] = row_in.load(
                pool, dst_row, A["dst"][s * SUPER * P:(s + 1) * SUPER * P].partition_broadcast(P))

        def edge_keys(s):
            dve.wait(edge_state["rows"], have_later)
            edge_state["rows_read"] = dve.chain(lambda e: e.scalar_tensor_tensor(
                key_row, src_row, float(N), dst_row, ALU.mult, ALU.add))
            if s + 1 < NS:
                load_edge_rows(s + 1)

        def edge_twins(s, j):
            c, width = s * SUPER + j, (SUPER - j) * P
            dve.chain(lambda e: e.scalar_tensor_tensor(
                same[:, 0:width], key_row[:, j * P:], ecol[:, 3, c:c + 1], later[:, 0:width],
                ALU.is_equal, ALU.mult, accum_out=ecol[:, 7, c:c + 1]))
            if j == SUPER - 1:
                cut = slice(s * SUPER, (s + 1) * SUPER)
                dve.chain(lambda e: e.scalar_tensor_tensor(ecol[:, 4, cut], ecol[:, 7, cut], 0.0,
                                                           ecol[:, 4, cut], ALU.is_equal, ALU.mult))

        edge_products = []

        def edge_chunk(c):
            o = c % 2
            while len(edge_products) > 1:
                edge_products.pop(0)()
            if c >= 2:
                dve.wait(edge_state[c - 2])
            dve.wait(have_node)
            dve.do(lambda e: e.tensor_scalar(onehot_src[:, o], node[:], ecol[:, 0, c:c + 1], None, ALU.is_equal))
            hot = dve.do(lambda e: e.tensor_scalar(onehot_dst[:, o], node[:], ecol[:, 1, c:c + 1],
                                                   ecol[:, 4, c:c + 1], ALU.is_equal, ALU.mult))

            def products():
                pe.wait(hot)
                for i in range(NT):
                    done = pe.do(lambda e, i=i: e.matmul(bank[i][:, 0:N], onehot_src[:, o, i * P:(i + 1) * P],
                                                         onehot_dst[:, o], start=(c == 0), stop=(c == EC - 1)))
                edge_state[c] = done
            edge_products.append(products)

        def edge_mask():
            while edge_products:
                edge_products.pop(0)()
            digits = k2_flat[:, 0:NT * N].rearrange("p (t n) -> p t n", t=NT)
            kind = k2_flat[:, NT * N:2 * NT * N].rearrange("p (t n) -> p t n", t=NT)
            dve.wait(edge_state[EC - 1], have_diag)
            for i in range(NT):
                last = dve.do(lambda e, i=i: e.tensor_tensor(digits[:, i], bank[i][:, 0:N], diag[:, i], ALU.max))
                read_by(i, last)
            dve.wait(last)
            dve.do(lambda e: e.tensor_scalar(mask8[:], digits, 0.0, 8.0 * ABSENT, ALU.is_equal, ALU.mult))
            dve.chain(lambda e: e.tensor_scalar(kind.bitcast(I32), digits.bitcast(I32), 23, 3,
                                                ALU.logical_shift_right, ALU.bitwise_and))
            for w, code in enumerate((3.0, 0.0, 1.0, 2.0)):
                dve.chain(lambda e, w=w, code=code: e.tensor_scalar(
                    digits, kind.bitcast(I32), code, etw[:, 5, w:w + 1], ALU.is_equal, ALU.mult))
                last = dve.chain(lambda e: e.tensor_tensor(mask8[:], mask8[:], digits, ALU.add))
            return last

        x_in, mid = Operand(in_hi, in_lo), Operand(mid_hi, mid_lo)
        normed = layer_norm(rows, lambda i, hh: (got_x,))
        transpose_rows(rows, normed, (3, 4, 5, 6, 7), x_in)
        load_edge_rows(0)

        def to_mid(col):
            def evacuate(k, bk, done):
                mid.ready[k] = split_out(bk, bank[bk][:, 0:N], mid_hi[:, k, :], mid_lo[:, k, :], done,
                                         bias=cols[:, col, k:k + 1])
                return mid.ready[k]
            return evacuate

        def to_plain(target, col):
            def evacuate(k, bk, done):
                act.wait(done)
                return act.do(lambda e: e.activation(target[:, k, :], bank[bk][:, 0:N], ACT.Identity,
                                                     bias=cols[:, col, k:k + 1]))
            return evacuate

        edge_work = [edge_weights, edge_values]
        for s in range(NS):
            edge_work.append(lambda s=s: edge_keys(s))
            edge_work += [lambda s=s, j=j: edge_twins(s, j) for j in range(SUPER)]
            edge_work += [lambda c=c: edge_chunk(c) for c in range(s * SUPER, (s + 1) * SUPER)]
        PROJECTIONS = ((x_in, to_mid(0)), (mid, to_plain(q2, 1)), (x_in, to_mid(2)), (x_in, None),
                       (mid, to_plain(k2, 3)), (x_in, to_mid(4)))
        SHADOW = 12
        share = -(-len(edge_work) // SHADOW)

        def between():
            for _ in range(share):
                if edge_work:
                    edge_work.pop(0)()

        act.wait(got_small)
        have_mask = None
        for operand, evacuate in PROJECTIONS:
            if evacuate is None:
                while edge_work:
                    edge_work.pop(0)()
                have_mask = edge_mask()
                act.wait(have_mask)
                sync.wait(have_mask)
                biv_in = bias_in.load(sync, row_bias, A["biv"].partition_broadcast(P))
                continue
            for c in range(2):
                for _ in product_cols(operand, c, evacuate):
                    between()

        def to_v2(c):
            def evacuate(i, bk, done):
                dve.wait(done, biv_in)
                return dve.do(lambda e: e.tensor_tensor(v2[:, i, c * HALF:(c + 1) * HALF], bank[bk][:],
                                                        row_bias[:, c * HALF:(c + 1) * HALF], ALU.add))
            return evacuate

        for c in range(2):
            product_rows(mid, to_v2(c), (0, 1, 2) if c else (3, 4, 5))
        have_v2 = (dve.sems[0], dve.counts[0])

        act.wait(have_v2)
        pe.wait((act.sems[0], act.counts[0]), have_v2)
        heads = [(h, i) for h in range(HEADS) for i in range(NT)]
        token = {}

        def scores(n):
            h, i = heads[n]
            base, k = (h % 2) * DH, h // 2
            bk = n % 3
            wait_bank(bk)
            token["s", n] = pe.do(lambda e: e.matmul(bank[bk][:, 0:N], q2[base:base + DH, k, i * P:(i + 1) * P],
                                                     k2[base:base + DH, k, :], start=True, stop=True))

        def softmax(n):
            bk, o, q, pb = n % 3, n % 2, n % 4, n % 3
            if n >= 2:
                dve.wait(token["e", n - 2])
            dve.wait(token["s", n], have_mask)
            m = dve.do(lambda e: e.tensor_tensor_reduce(
                out=score[:, o], in0=bank[bk][:, 0:N], in1=mask8[:, heads[n][1]],
                scale=-1.0 / 8.0, scalar=3.0e38, op0=ALU.add, op1=ALU.min, accum_out=sums[:, q, 0:1]))
            read_by(bk, m)
            act.wait(m)
            if n >= 3:
                act.wait(token["t", n - 3])
            token["e", n] = act.do(lambda e: e.activation(prob[:, pb], score[:, o], ACT.Exp, scale=-1.0,
                                                          bias=sums[:, q, 0:1], accum_out=sums[:, q, 1:2]))

        def normalise(n):
            q, pb = n % 4, n % 3
            dve.wait(token["e", n])
            dve.chain(lambda e: e.reciprocal(sums[:, q, 1:2], sums[:, q, 1:2]))
            token["p", n] = dve.do(lambda e: e.tensor_scalar(prob[:, pb], prob[:, pb], sums[:, q, 1:2], None,
                                                             ALU.mult))

        def turn_probabilities(n):
            h, i = heads[n]
            bk, o = 3 + n % 2, n % 3
            wait_bank(bk)
            pe.wait(token["p", n])
            for m in range(NT):
                step = (lambda e, m=m: e.transpose(bank[bk][:, m * P:(m + 1) * P],
                                                   prob[:, o, m * P:(m + 1) * P], ident[:]))
                done = pe.do(step)
            token["t", n] = done
            act.wait(done)
            if h >= 2:
                act.wait(token["o", h - 2])
            token["c", n] = act.do(lambda e: e.activation(
                prob_t[:, h % 2, :, i * P:(i + 1) * P],
                bank[bk][:, 0:N].rearrange("p (m n) -> p m n", m=NT), ACT.Copy))
            read_by(bk, token["c", n])

        def attend(h):
            bk = 5 + (h // 2) % 2
            base = (h % 2) * DH
            if h % 2 == 0:
                wait_bank(bk)
            pe.wait(token["c", NT * h + NT - 1])
            for m in range(NT):
                done = pe.do(lambda e, m=m: e.matmul(bank[bk][base:base + DH, 0:N], v2[:, m, h * DH:(h + 1) * DH],
                                                     prob_t[:, h % 2, m, :], start=(m == 0), stop=(m == NT - 1)))
            token["o", h] = done
            if h % 2:
                x_in.ready[h // 2] = split_out(bk, bank[bk][:, 0:N], in_hi[:, h // 2, :], in_lo[:, h // 2, :], done)

        AHEAD = 2
        for n in range(len(heads) + AHEAD + 1):
            if n < len(heads):
                scores(n)
            if n >= AHEAD and n - AHEAD < len(heads):
                turn_probabilities(n - AHEAD)
                if heads[n - AHEAD][1] == NT - 1 and heads[n - AHEAD][0] > 0:
                    attend(heads[n - AHEAD][0] - 1)
            if n < len(heads):
                softmax(n)
            if 1 <= n <= len(heads):
                normalise(n - 1)
        attend(HEADS - 1)

        pool.wait(token["s", len(heads) - 1], token["o", HEADS - 1])
        bo_in = Arrival(sem("bo_in")).load(pool, row_bias, A["bo"].partition_broadcast(P))
        got_x = Arrival(sem("x_again_in")).load(pool, x_again, A["x"].rearrange("(t p) d -> p t d", p=P))

        def to_residual(c):
            cut = slice(c * HALF, (c + 1) * HALF)

            def evacuate(i, bk, done):
                dve.wait(done, bo_in, got_x)
                part = dve.do(lambda e: e.tensor_tensor(x_rows[:, i, cut], bank[bk][:], row_bias[:, cut], ALU.add))
                dve.wait(part)
                token["x", i, c] = dve.do(lambda e: e.tensor_tensor(x_rows[:, i, cut], x_rows[:, i, cut],
                                                                   x_again[:, i, cut], ALU.add))
                return part
            return evacuate

        for c in range(2):
            product_rows(x_in, to_residual(c), (0, 1, 2) if c else (3, 4, 7))

        graph_done = token["x", NT - 1, 1]
        act.wait(graph_done)
        small.load(act, router_raw[:], A["router"].rearrange("(k p) e -> p k e", p=P))
        got_router = small.load(act, e_bias[:], A["e_bias"].partition_broadcast(P))
        normed = layer_norm(rows2, lambda i, hh: (token["x", i, hh],))
        act.wait(got_router)
        dve.wait(got_router)
        hi = act.do(lambda e: e.activation(router_hi[:], router_raw[:], ACT.Copy))
        dve.wait(hi)
        have_router = dve.do(lambda e: e.tensor_tensor(router_lo[:], router_raw[:], router_hi[:].bitcast(F32),
                                                       ALU.subtract))
        transpose_rows(rows2, normed, (5, 6, 7), x_in)
        rows_out = Arrival(sem("rows_out"))
        pool.wait(*normed)
        rows_out.load(pool, normed_dram.rearrange("(t p) d -> p t d", p=P), rows2[:])
        have_normed = rows_out.load(pool, out[N:N + P, :], rows2[:, 0, :])

        pool.do(lambda e: e.memset(ones16[:], 1.0))
        pool.do(lambda e: e.memset(before[:], 1.0))
        pool.chain(lambda e: e.memset(earlier[:], 1.0))
        pool.do(lambda e: e.affine_select(
            out=earlier[:], in_=earlier[:], compare_op=ALU.is_gt, fill=0.0, base=0,
            pattern=[[1, EXPERTS], [-1, EXPERTS]], channel_multiplier=0))
        pool.do(lambda e: e.affine_select(out=before[:], in_=before[:], compare_op=ALU.is_gt, fill=0.0, base=0,
                                          pattern=[[1, P]], channel_multiplier=-1))
        pool.do(lambda e: e.iota(slot[:], pattern=[[1, N]], base=0, channel_multiplier=0,
                                 allow_small_or_imprecise_dtypes=True))
        pool.do(lambda e: e.iota(token_id[:], pattern=[[P, NT]], base=0, channel_multiplier=1,
                                 allow_small_or_imprecise_dtypes=True))
        have_tables = pool.do(lambda e: e.iota(spare_row[:, 0:1], pattern=[[0, 1]], base=N, channel_multiplier=1,
                                               allow_small_or_imprecise_dtypes=True))

        wait_bank(0)
        pe.wait(have_router)
        for i in range(NT):
            for k in range(KT):
                pe.wait(*x_in.when(k, i))
                for m, (a, w) in enumerate(PASSES):
                    step = (lambda e, i=i, k=k, m=m, a=a, w=w: e.matmul(
                        bank[0][:, i * EXPERTS:(i + 1) * EXPERTS],
                        (x_in.hi, x_in.lo)[a][:, k, i * P:(i + 1) * P],
                        (router_hi, router_lo)[w][:, k, :], start=(k == 0 and m == 0),
                        stop=(k == KT - 1 and m == 2)))
                    if k == KT - 1 and m == 2:
                        done = pe.do(step)
                    else:
                        pe.run(step)
        act.wait(done)
        sig = act.do(lambda e: e.activation(
            prob_e[:], bank[0][:, 0:NT * EXPERTS].rearrange("p (t e) -> p t e", t=NT), ACT.Sigmoid))
        read_by(0, sig)

        biased, masked, chosen, tmp = r
        four = biased[:].rearrange("p t (g s) -> p t g s", s=GSIZE)

        def group_scores():
            dve.wait(sig, got_router, have_tables)
            for i in range(NT):
                last = dve.do(lambda e, i=i: e.tensor_tensor(biased[:, i], prob_e[:, i], e_bias[:], ALU.add))
            dve.wait(last)
            a_, b_, c_, d_ = (four[:, :, :, j] for j in range(GSIZE))
            dve.do(lambda e: e.tensor_tensor(gs[:, :, 0], a_, b_, ALU.max))
            dve.do(lambda e: e.tensor_tensor(gs[:, :, 1], a_, b_, ALU.min))
            dve.do(lambda e: e.tensor_tensor(gs[:, :, 2], c_, d_, ALU.max))
            dve.chain(lambda e: e.tensor_tensor(gs[:, :, 3], c_, d_, ALU.min))
            dve.do(lambda e: e.tensor_tensor(gs[:, :, 4], gs[:, :, 0], gs[:, :, 2], ALU.max))
            dve.do(lambda e: e.tensor_tensor(gs[:, :, 5], gs[:, :, 0], gs[:, :, 2], ALU.min))
            dve.chain(lambda e: e.tensor_tensor(gs[:, :, 1], gs[:, :, 1], gs[:, :, 3], ALU.max))
            dve.chain(lambda e: e.tensor_tensor(gs[:, :, 5], gs[:, :, 5], gs[:, :, 1], ALU.max))
            dve.chain(lambda e: e.tensor_tensor(gs[:, :, 0], gs[:, :, 4], gs[:, :, 5], ALU.add))

        def rank_of(values, n, result):
            rival = values.unsqueeze(1).to_broadcast([P, n, n])
            own = values.unsqueeze(2).to_broadcast([P, n, n])
            bb, b2 = beats[:, 0:n, 0:n], beats2[:, 0:n, 0:n]
            dve.do(lambda e: e.tensor_tensor(bb, rival, own, ALU.is_gt))
            dve.chain(lambda e: e.tensor_tensor(b2, rival, own, ALU.is_equal))
            dve.chain(lambda e: e.tensor_tensor(b2, b2, earlier[:, 0:n, 0:n], ALU.mult))
            dve.chain(lambda e: e.tensor_tensor(bb, bb, b2, ALU.add))
            dve.chain(lambda e: e.tensor_reduce(result, bb, AX.X, ALU.add))

        def mask_groups():
            dve.chain(lambda e: e.tensor_scalar(gs[:, :, 2], gs[:, :, 1], 1.5, None, ALU.is_lt))
            dve.chain(lambda e: e.tensor_scalar(gs[:, :, 3], gs[:, :, 2], -1.0, None, ALU.add))
            for i in range(NT):
                inside = gs[:, i, 2].unsqueeze(2).to_broadcast([P, GROUPS, GSIZE])
                less = gs[:, i, 3].unsqueeze(2).to_broadcast([P, GROUPS, GSIZE])
                grouped = masked[:, i].rearrange("p (g s) -> p g s", s=GSIZE)
                dve.chain(lambda e, i=i, inside=inside, grouped=grouped: e.tensor_tensor(
                    grouped, four[:, i], inside, ALU.mult))
                dve.chain(lambda e, less=less, grouped=grouped: e.tensor_tensor(grouped, grouped, less, ALU.add))

        def weigh():
            dve.chain(lambda e: e.tensor_scalar(chosen[:], tmp[:], GSIZE - 0.5, None, ALU.is_lt))
            token["chosen"] = dve.do(lambda e: e.tensor_copy(chosen16[:], chosen[:]))
            dve.chain(lambda e: e.tensor_tensor(tmp[:], chosen[:], prob_e[:], ALU.mult))
            dve.chain(lambda e: e.tensor_reduce(denom[:], tmp[:], AX.X, ALU.add))
            dve.chain(lambda e: e.tensor_scalar(denom[:], denom[:], 1e-20, None, ALU.add))
            dve.chain(lambda e: e.reciprocal(denom[:], denom[:]))
            for i in range(NT):
                last = dve.do(lambda e, i=i: e.tensor_scalar(combine[:, i], tmp[:, i], denom[:, i:i + 1],
                                                             ROUTE_SCALE, ALU.mult, ALU.mult))
            dve.wait(last)

        def place_tokens():
            pe.wait(token["chosen"], have_tables)
            wait_bank(6)
            for i in range(NT + 1):
                terms = [(ones16, j) for j in range(min(i, NT))] + ([(before, i)] if i < NT else [])
                for n, (lhs, j) in enumerate(terms):
                    done = pe.do(lambda e, i=i, lhs=lhs, j=j, n=n, last=len(terms) - 1: e.matmul(
                        bank[6][:, i * EXPERTS:(i + 1) * EXPERTS], lhs[:], chosen16[:, j],
                        start=(n == 0), stop=(n == last)))
            token["placed"] = done

        def use_places():
            dve.wait(token["placed"])
            got = dve.do(lambda e: e.tensor_copy(
                place[:], bank[6][:, 0:(NT + 1) * EXPERTS].rearrange("p (t e) -> p t e", e=EXPERTS)))
            read_by(6, got)
            dve.wait(got)
            token["counts"] = dve.do(lambda e: e.tensor_copy(counts[:], place[:, NT]))
            dve.chain(lambda e: e.tensor_tensor(place[:, 0:NT], place[:, 0:NT], chosen[:], ALU.mult))
            dve.chain(lambda e: e.tensor_tensor(place[:, 0:NT], place[:, 0:NT], chosen[:], ALU.add))
            dve.chain(lambda e: e.tensor_scalar(place[:, 0:NT], place[:, 0:NT], -1.0, None, ALU.add))
            dve.do(lambda e: e.tensor_copy(info[:, :, :, 0], token_id[:].unsqueeze(2).to_broadcast(
                [P, NT, EXPERTS])))
            dve.do(lambda e: e.tensor_scalar(info[:, :, :, 1], combine[:], 0.0, 1.0, ALU.mult, ALU.add))
            dve.chain(lambda e: e.tensor_copy(info[:, :, :, 2], combine[:]))
            dve.chain(lambda e: e.tensor_tensor(info[:, :, :, 3], combine[:], info[:, :, :, 2].bitcast(F32),
                                                ALU.subtract))

        def choose(x):
            if x:
                dve.wait(token["slots", x - 1])
            for i in range(NT):
                hot = dve.do(lambda e, i=i: e.tensor_scalar(chooses[:, i], slot[:], place[:, i, x:x + 1], None,
                                                            ALU.is_equal))

            def products():
                pe.wait(hot)
                wait_bank(7)
                for j in range(NT):
                    for i in range(NT):
                        done = pe.do(lambda e, i=i, j=j: e.matmul(
                            bank[7][:, j * 4:j * 4 + 4], chooses[:, i, j * P:(j + 1) * P], info[:, i, x, :],
                            start=(i == 0), stop=(i == NT - 1)))
                token["slots", x] = done
                dve.wait(done)
                read_by(7, dve.do(lambda e: e.tensor_copy(
                    slots[:, x * NT:(x + 1) * NT], bank[7][:, 0:NT * 4].rearrange("p (s c) -> p s c", c=4))))
            return products

        def slot_tables():
            dve.chain(lambda e: e.tensor_scalar(spare_row[:, 1:2], spare_row[:, 0:1], -1.0, None, ALU.mult))
            dve.do(lambda e: e.tensor_copy(gather_at[:], slots[:, :, 0]))
            dve.do(lambda e: e.tensor_tensor(slot_w[:], slots[:, :, 2], slots[:, :, 3], ALU.add))
            dve.chain(lambda e: e.tensor_scalar(slot_to[:], slots[:, :, 1], spare_row[:, 1:2], spare_row[:, 0:1],
                                                ALU.mult, ALU.add))
            dve.chain(lambda e: e.tensor_tensor(slot_to[:], slot_to[:], slots[:, :, 0], ALU.add))
            token["tables"] = dve.do(lambda e: e.tensor_copy(scatter_at[:], slot_to[:]))

        side = [group_scores]
        side += [lambda i=i: rank_of(gs[:, i, 0], GROUPS, gs[:, i, 1]) for i in range(NT)]
        side += [mask_groups]
        side += [lambda i=i: rank_of(masked[:, i], EXPERTS, tmp[:, i]) for i in range(NT)]
        side += [weigh, lambda: (place_tokens(), use_places())]
        side += [lambda x=x: side.insert(0, choose(x)) for x in range(EXPERTS)]
        side += [slot_tables]

        registers = {}

        def load_counts():
            for lane in (pe, act, dve, pool):
                lane.wait(token["counts"])

                def load(e, lane=lane):
                    registers[id(lane)] = [e.value_load(counts[0:1, x:x + 1], min_val=0, max_val=N)
                                           for x in range(EXPERTS)]
                lane.run(load)

        gathered = [Arrival(sem(f"gathered{t}")) for t in range(NT)]
        scattered = [Arrival(sem(f"scattered{t}")) for t in range(NT)]

        indirect = (*gathered, *scattered)

        @contextmanager
        def section(x, t):
            lanes = (pe, act, dve, pool)
            kept = [(lane.steps, lane.track, dict(lane.waited), list(lane.counts)) for lane in lanes]
            arrivals = [a.count for a in indirect]
            for lane in lanes:
                lane.steps, lane.track = [], t
            yield
            for lane, (steps, track, waited, counts_before) in zip(lanes, kept):
                body, lane.steps, lane.track, lane.waited = lane.steps, steps, track, waited
                if not body:
                    continue
                missing = [(s_, was, now - was)
                           for s_, was, now in zip(lane.sems, counts_before, lane.counts) if now > was]
                unsent = [(a.sem, was, n) for n, (a, was) in enumerate(zip(indirect, arrivals))
                          if lane is pool and a.count > was]

                def branch(e, lane=lane, body=body, missing=missing, unsent=unsent):
                    with e.If(registers[id(lane)][x] > t * P):
                        for step in body:
                            step(e)
                    with e.Else():
                        for s_, was, n in missing:
                            if was:
                                e.wait_ge(s_, was)
                            e.sem_inc(s_, n)
                        for s_, was, n in unsent:
                            if was:
                                e.wait_ge(s_, was)
                            e.dma_start(idle[:, n:n + 1], ident[0:1, 0:1]).then_inc(s_, 16)
                lane.run(branch)

        def each_tile(u, work):
            work(0)
            if u < SHARED:
                work(1)
                work(2)
            else:
                with section(u - SHARED, 1):
                    work(1)
                    with section(u - SHARED, 2):
                        work(2)

        def gather(x, t):
            n = x * NT + t
            pool.wait(token["tables"], have_normed)
            if ("turned x", t) in token:
                pool.wait(token["turned x", t])
            token["gathered", t] = gathered[t].start(pool, lambda e: e.indirect_dma_start(
                out=rows2[:, t, :], out_offset=None, in_=normed_dram,
                in_offset=bass.IndirectOffsetOnAxis(ap=gather_at[:, n:n + 1], axis=0)))

        def turn_x(t):
            pe.wait(token["gathered", t])
            for b in range(2):
                bk = 6 + b
                wait_bank(bk)
                for m in range(HALF // P):
                    step = (lambda e, b=b, m=m, bk=bk: e.transpose(
                        bank[bk][:, m * P:(m + 1) * P], rows2[:, t, (4 * b + m) * P:(4 * b + m + 1) * P],
                        ident[:]))
                    if m == HALF // P - 1:
                        done = pe.do(step)
                    else:
                        pe.run(step)
                ks, ts = slice(4 * b, 4 * b + 4), slice(t * P, (t + 1) * P)
                got = split_out(bk, bank[bk][:].rearrange("p (k n) -> p k n", n=P),
                                in_hi[:, ks, ts], in_lo[:, ks, ts], done)
                for k in range(4 * b, 4 * b + 4):
                    x_in.ready[k, t] = got
            token["turned x", t] = done

        hid = Operand(act_hi, act_lo)

        def turn_hidden(c, t):
            bk = 6 + (t + c) % 2
            pe.wait(token["hidden", t])
            wait_bank(bk)
            for m in range(HALF // P):
                step = (lambda e, m=m: e.transpose(bank[bk][:, m * P:(m + 1) * P],
                                                   hidden[:, t, m * P:(m + 1) * P], ident[:]))
                if m == HALF // P - 1:
                    done = pe.do(step)
                else:
                    pe.run(step)
            token["hidden turned", t] = done
            ks, ts = slice(4 * c, 4 * c + 4), slice(t * P, (t + 1) * P)
            got = split_out(bk, bank[bk][:].rearrange("p (k n) -> p k n", n=P),
                            act_hi[:, ks, ts], act_lo[:, ks, ts], done)
            for k in range(4 * c, 4 * c + 4):
                hid.ready[k, t] = got

        GATE_BANK, UP_BANK = (0, 4, 5), (1, 4, 5)
        DOWN_BANKS = ((2, 3), (4, 5), (0, 1))

        def stage(u, s):
            (t0, ready0), (t1, ready1) = next_piece(SPLIT), next_piece(SPLIT - 1)
            pe.wait(*ready0)
            c = s // 2

            def tile(t):
                if s < 4:
                    bk = (GATE_BANK, UP_BANK)[s % 2][t]
                    rows_piece(x_in, t, t0, 0, bk)
                    if t == 0:
                        pe.wait(*ready1)
                    done = rows_piece(x_in, t, t1, 1, bk)
                    if s % 2 == 0:
                        act.wait(done)
                        if ("hidden", t) in token:
                            act.wait(token["hidden", t])
                        token["silu", t] = act.do(lambda e: e.activation(gated[:, t], bank[bk][:], ACT.Silu))
                        read_by(bk, token["silu", t])
                    else:
                        dve.wait(done, token["silu", t])
                        if ("hidden turned", t) in token:
                            dve.wait(token["hidden turned", t])
                        token["hidden", t] = dve.do(lambda e: e.tensor_tensor(hidden[:, t], bank[bk][:],
                                                                              gated[:, t], ALU.mult))
                        read_by(bk, token["hidden", t])
                    if s == 2:
                        turn_hidden(0, t)
                else:
                    kh = s - 4
                    done = []
                    for half, piece_slot in enumerate((t0, t1)):
                        if t == 0 and half:
                            pe.wait(*ready1)
                        done.append(rows_piece(hid, t, piece_slot, kh, DOWN_BANKS[t][half]))
                    if s == 4:
                        turn_hidden(1, t)
                    else:
                        for half in range(2):
                            down_out(u, t, half, DOWN_BANKS[t][half], done[half])
            each_tile(u, tile)
            last = [(s_, n) for s_, n in zip(pe.sems, pe.counts) if n]
            split_free[t0] = split_free[t1] = last

        def down_out(u, t, half, bk, done):
            cut = slice(half * HALF, (half + 1) * HALF)
            if u < SHARED:
                dve.wait(done)
                token["x", t, half] = dve.do(lambda e: e.tensor_tensor(x_rows[:, t, cut], bank[bk][:],
                                                                      x_rows[:, t, cut], ALU.add))
                read_by(bk, token["x", t, half])
            else:
                n = (u - SHARED) * NT + t
                act.wait(done, token["base"])
                if scattered[t].count:
                    act.wait((scattered[t].sem, scattered[t].count))
                token["y", t] = act.do(lambda e: e.activation(x_rows[:, t, cut], bank[bk][:], ACT.Copy,
                                                              scale=slot_w[:, n:n + 1]))
                read_by(bk, token["y", t])

        def scatter(x, t):
            n = x * NT + t
            pool.wait(token["y", t], token["base"])
            pool.wait(*((a.sem, a.count) for a in scattered if a.count))
            scattered[t].start(pool, lambda e: e.indirect_dma_start(
                out=out, out_offset=bass.IndirectOffsetOnAxis(ap=scatter_at[:, n:n + 1], axis=0),
                in_=x_rows[:, t, :], in_offset=None, compute_op=ALU.add))

        def side_work(n):
            for _ in range(n):
                if side:
                    side.pop(0)()

        base_out = Arrival(sem("base_out"))
        for u in range(UNITS):
            x = u - SHARED
            for s in range(6):
                if x + 1 >= 0 and x + 1 < EXPERTS and s == 4:
                    if x + 1 == 0:
                        while side:
                            side.pop(0)()
                        load_counts()
                        each_tile(u + 1, lambda t: gather(0, t))
                stage(u, s)
                side_work(5)
                if s == 4 and x + 1 >= 0 and x + 1 < EXPERTS:
                    each_tile(u + 1, turn_x)
                    if x + 2 < EXPERTS:
                        each_tile(u + 2, lambda t: gather(x + 2, t))
            if x >= 0:
                each_tile(u, lambda t: scatter(x, t))
            elif u == SHARED - 1:
                pool.wait(*(token["x", t, half] for t in range(NT) for half in range(2)))
                token["base"] = base_out.load(pool, out[0:N, :].rearrange("(t p) d -> p t d", p=P), x_rows[:])
                pool.wait(token["base"])
        assert taken[0] == len(pieces)

        sync.wait(*((a.sem, a.count) for a in scattered), token["base"], have_normed)

        block = ctx.enter_context(nc.Block())
        block.sync(sync.emit)
        block.gpsimd(pool.emit)
        block.scalar(act.emit)
        block.vector(dve.emit)
        block.tensor(pe.emit)


def kernel(**inputs):
    import concourse.bacc as bacc
    from concourse.bass_utils import run_bass_kernel_spmd

    def get(name):
        return np.ascontiguousarray(inputs[name])

    def columns(v):
        return np.ascontiguousarray(v.reshape(-1, P).T)

    arrays = {"x": get("x"), "src": get("src"), "dst": get("dst"),
              "src_cols": columns(get("src")), "dst_cols": columns(get("dst")),
              "type_cols": columns(get("edge_type_5")), "etw": get("L0_gnn_edge_type_weights")}
    for name in ("wq", "wk", "wv", "wiq", "wik", "wiv", "wo"):
        arrays[name] = np.ascontiguousarray(get("L0_gnn_" + name).T)
    for name in ("bq", "bk", "bv", "biq", "bik"):
        arrays[name] = columns(get("L0_gnn_" + name))
    arrays.update(biv=get("L0_gnn_biv"), bo=get("L0_gnn_bo"),
                  router=np.ascontiguousarray(get("L0_ffn_router_w").T), e_bias=get("L0_ffn_bias"),
                  gate=get("L0_ffn_gate_w"), up=get("L0_ffn_up_w"), down=get("L0_ffn_down_w"),
                  sh_gate=get("L0_ffn_sh_gate_w"), sh_up=get("L0_ffn_sh_up_w"),
                  sh_down=get("L0_ffn_sh_down_w"))

    nc = bacc.Bacc("TRN2", target_bir_lowering=False, num_devices=1)
    aps = {name: nc.dram_tensor("in_" + name, a.shape, mybir.dt.from_np(a.dtype), kind="ExternalInput").ap()
           for name, a in arrays.items()}
    normed = nc.dram_tensor("normed", (N, D), F32, kind="Internal").ap()
    out = nc.dram_tensor("result", (N + P, D), F32, kind="ExternalOutput").ap()
    build(nc, aps, normed, out)
    ran = run_bass_kernel_spmd(nc, [{"in_" + name: a for name, a in arrays.items()}], core_ids=[0])
    return ran.results[0]["result"][:N]
```

```python
from contextlib import ExitStack, contextmanager

import numpy as np
import concourse.bass as bass
from concourse import mybir
from concourse.alu_op_type import AluOpType as ALU

F32 = mybir.dt.float32
F32R = mybir.dt.float32r
BF16 = mybir.dt.bfloat16
I32 = mybir.dt.int32
ACT = mybir.ActivationFunctionType
AX = mybir.AxisListType

P = 128
N = 384
NT = N // P
D = 1024
KT = D // P
HEADS = 16
DH = D // HEADS
EDGES = 6144
EC = EDGES // P
SUPER = 8
NS = EC // SUPER
ONEHOTS = 5
EXPERTS = 16
GROUPS = 4
GSIZE = EXPERTS // GROUPS
SHARED = 2
ROUTE_SCALE = 2.5
EPS = 1e-5
ABSENT = -1.0e30

HALF = 512
KPIECE = 4
RAW = 4
MORE_RAW = 1
FACTS = 6
SPLIT = 4


class Lane:

    def __init__(self, sems):
        self.sems, self.track = sems, 0
        self.counts, self.steps, self.waited = [0] * len(sems), [], {}

    def wait(self, *tokens):
        for sem, value in tokens:
            if self.waited.get(id(sem), 0) < value:
                self.waited[id(sem)] = value
                self.steps.append(lambda e, s=sem, v=value: e.wait_ge(s, v))

    def run(self, step):
        self.steps.append(step)

    def do(self, step):
        sem = self.sems[self.track]
        self.counts[self.track] += 1
        self.steps.append(lambda e: step(e).then_inc(sem, 1))
        return sem, self.counts[self.track]

    def chain(self, step):
        done = self.do(step)
        self.wait(done)
        return done

    def emit(self, engine):
        for step in self.steps:
            step(engine)


class Arrival:

    def __init__(self, sem):
        self.sem, self.count = sem, 0

    def load(self, lane, out, in_):
        return self.start(lane, lambda e: e.dma_start(out, in_))

    def start(self, lane, step):
        self.count += 16
        lane.run(lambda e: step(e).then_inc(self.sem, 16))
        return self.sem, self.count


class Operand:

    def __init__(self, hi, lo):
        self.hi, self.lo, self.ready = hi, lo, {}

    def when(self, k, i):
        return [self.ready[x] for x in (k, (k, i)) if x in self.ready]


def build(nc, A, normed_dram, out):
    with ExitStack() as ctx, ExitStack() as gnn_buffers:
        def sb(name, shape, dt=F32, scope=ctx):
            return scope.enter_context(nc.sbuf_tensor(name, shape, dt))

        def sem(name):
            return ctx.enter_context(nc.semaphore(name))

        bank = [ctx.enter_context(nc.psum_tensor(f"bank{i}", [P, HALF], F32)) for i in range(8)]
        bank_read = [{} for _ in range(8)]

        raw = sb("raw", [P, RAW, KPIECE, HALF])
        w_hi = sb("w_hi", [P, SPLIT, KPIECE, HALF], F32R)
        w_lo = sb("w_lo", [P, SPLIT, KPIECE, HALF], F32R)
        in_hi = sb("in_hi", [P, KT, N], F32R)
        in_lo = sb("in_lo", [P, KT, N], F32R)
        x_rows = sb("x_rows", [P, NT, D])
        ident = sb("ident", [P, P])
        stats = sb("stats", [P, NT, 2, 6])
        meanvar = sb("meanvar", [P, NT, 2])
        rstd = sb("rstd", [P, NT])
        half_neg = sb("half_neg", [P, NT])
        warm = sb("warm", [P, NT])
        cols = sb("cols", [P, 5, KT])

        router_raw = sb("router_raw", [P, KT, EXPERTS])
        router_hi = sb("router_hi", [P, KT, EXPERTS], F32R)
        router_lo = sb("router_lo", [P, KT, EXPERTS], F32R)
        e_bias = sb("e_bias", [P, EXPERTS])

        g = gnn_buffers
        mid_hi = sb("mid_hi", [P, KT, N], F32R, g)
        mid_lo = sb("mid_lo", [P, KT, N], F32R, g)
        q2 = sb("q2", [P, KT, N], F32, g)
        rows = q2[:].rearrange("p k n -> p (k n)").rearrange("p (t d) -> p t d", t=NT)
        k2 = sb("k2", [P, KT, N], F32, g)
        k2_flat = k2[:].rearrange("p k n -> p (k n)")
        x_again = k2_flat.rearrange("p (t d) -> p t d", t=NT)
        v2 = x_rows
        mask8 = sb("mask8", [P, NT, N], F32, g)
        low = sb("low", [P, 4], F32, g)
        sums = sb("sums", [P, 2, HEADS], F32, g)
        etw = sb("etw", [P, 6, 4], F32, g)
        with ExitStack() as edge_buffers:
            b = edge_buffers
            src_row = k2_flat[:, 0:SUPER * P].bitcast(I32)
            dst_row = k2_flat[:, SUPER * P:2 * SUPER * P].bitcast(I32)
            key_row = k2_flat[:, 2 * SUPER * P:3 * SUPER * P]
            later = sb("later", [P, SUPER * P], BF16, b)
            same = sb("same", [P, SUPER * P], BF16, b)
            onehot_src = sb("onehot_src", [P, ONEHOTS, N], BF16, b)
            onehot_dst = sb("onehot_dst", [P, ONEHOTS, N], BF16, b)
            node = sb("node", [P, N], F32, b)
            diag = sb("diag", [P, NT, N], F32, b)
            ecol_i = sb("ecol_i", [P, 3, EC], I32, b)
            ecol = sb("ecol", [P, 8, EC], F32, b)
        with ExitStack() as attention_buffers:
            b = attention_buffers
            score = sb("score", [P, 2, N], F32, b)
            prob = sb("prob", [P, 4, N], F32, b)
            prob_t = sb("prob_t", [P, 2, NT, P], F32, b)
            attended = sb("attended", [P, 2, HALF], F32, b)
            row_bias = sb("row_bias", [P, D], F32, b)
        gnn_buffers.close()

        act_hi = sb("act_hi", [P, KT, N], F32R)
        act_lo = sb("act_lo", [P, KT, N], F32R)
        rows2 = sb("rows2", [P, NT, D])
        gated = sb("gated", [P, NT, HALF])
        hidden = sb("hidden", [P, NT, HALF])
        prob_e = sb("prob_e", [P, NT, EXPERTS])
        r = [sb(f"route{i}", [P, NT, EXPERTS]) for i in range(4)]
        gs = sb("gs", [P, NT, 6, GROUPS])
        beats = sb("beats", [P, EXPERTS, EXPERTS])
        beats2 = sb("beats2", [P, EXPERTS, EXPERTS])
        earlier = sb("earlier", [P, EXPERTS, EXPERTS])
        combine = sb("combine", [P, NT, EXPERTS])
        denom = sb("denom", [P, NT])
        chosen16 = sb("chosen16", [P, NT, EXPERTS], BF16)
        before = sb("before", [P, P], BF16)
        ones16 = sb("ones16", [P, P], BF16)
        place = sb("place", [P, NT + 1, EXPERTS])
        slot = sb("slot", [P, N])
        tile_start = sb("tile_start", [P, NT])
        row_in_tile = sb("row_in_tile", [P, NT])
        info = sb("info", [P, NT, EXPERTS, FACTS], BF16)
        weight_rest = sb("weight_rest", [P, NT, EXPERTS])
        chooses = sb("chooses", [P, 2, NT, N], BF16)
        slots = sb("slots", [P, EXPERTS * NT, FACTS])
        slot_from = sb("slot_from", [P, EXPERTS * NT])
        spare_row = sb("spare_row", [P, 2])
        slot_w = sb("slot_w", [P, EXPERTS * NT])
        slot_to = sb("slot_to", [P, EXPERTS * NT])
        gather_at = sb("gather_at", [P, EXPERTS * NT], I32)
        scatter_at = sb("scatter_at", [P, EXPERTS * NT], I32)
        more = sb("more", [P, NT - 1, EXPERTS])
        bits = sb("bits", [P, NT - 1, EXPERTS])
        words_f = sb("words_f", [P, NT - 1])
        words = sb("words", [P, NT - 1], I32)
        idle = sb("idle", [1, 2 * NT])
        more_raw = sb("more_raw", [P, MORE_RAW, KPIECE, HALF])

        pe, act, dve, pool = (Lane([sem(f"{n}_done{t or ''}") for t in range(NT)])
                              for n in ("tensor", "scalar", "vector", "gpsimd"))
        sync = Lane([None])
        raw_in = [Arrival(sem(f"raw_in{i}")) for i in range(RAW + MORE_RAW)]

        def read_by(bk, *tokens):
            if pe.track == 0:
                bank_read[bk] = {}
            for s_, v in tokens:
                bank_read[bk][id(s_)] = (s_, v)

        def wait_bank(bk):
            pe.wait(*bank_read[bk].values())

        pieces = []
        raw_slots = [raw[:, i] for i in range(RAW)] + [more_raw[:, i] for i in range(MORE_RAW)]
        raw_free = [None] * len(raw_slots)
        split_free = [[]] * SPLIT

        def piece(w, c, kh):
            return w.rearrange("(k p) f -> p k f", p=P)[:, kh * KPIECE:(kh + 1) * KPIECE,
                                                        c * HALF:(c + 1) * HALF]

        for w in ("wq", "wiq", "wk", "wik", "wv", "wiv", "wo"):
            pieces += [piece(A[w], c, kh) for c in range(2) for kh in range(2)]

        def unit_matrices(u):
            if u < SHARED:
                cut = slice(u * D, (u + 1) * D)
                return A["sh_gate"][:, cut], A["sh_up"][:, cut], A["sh_down"][cut, :]
            return A["gate"][u - SHARED], A["up"][u - SHARED], A["down"][u - SHARED]

        UNITS = SHARED + EXPERTS
        for u in range(UNITS):
            gate, up, down = unit_matrices(u)
            for c in range(2):
                pieces += [piece(w, c, kh) for w in (gate, up) for kh in range(2)]
            pieces += [piece(down, c, kh) for kh in range(2) for c in range(2)]

        LONG_FROM = (7 * 4 // RAW + 1) * RAW
        loaded, high, low_parts, taken = [], [], [], [0]

        def raw_slot(i):
            return i % RAW if i < LONG_FROM else (i - LONG_FROM) % (RAW + MORE_RAW)

        def load_ahead(upto):
            while len(loaded) < min(upto, len(pieces)):
                i = len(loaded)
                s = raw_slot(i)
                if i == LONG_FROM + RAW:
                    sync.wait(*graph_over)
                if raw_free[s]:
                    sync.wait(raw_free[s])
                loaded.append(raw_in[s].load(sync, raw_slots[s], pieces[i]))

        def split_high(upto):
            while len(high) < min(upto, len(pieces)):
                i = len(high)
                load_ahead(i + 1)
                s, t = raw_slot(i), i % SPLIT
                act.wait(loaded[i], *split_free[t])
                high.append(act.do(lambda e, s=s, t=t: e.activation(w_hi[:, t], raw_slots[s], ACT.Copy)))

        def split_low(upto):
            while len(low_parts) < min(upto, len(pieces)):
                i = len(low_parts)
                s, t = raw_slot(i), i % SPLIT
                dve.wait(high[i])
                raw_free[s] = dve.do(lambda e, s=s, t=t: e.tensor_tensor(
                    w_lo[:, t], raw_slots[s], w_hi[:, t].bitcast(F32), ALU.subtract))
                low_parts.append(raw_free[s])
                load_ahead(i + 1 + RAW + (MORE_RAW if i >= LONG_FROM else 0))

        def split_ahead(upto):
            split_high(upto)
            split_low(upto)

        def next_piece(ahead=0):
            i = taken[0]
            taken[0] += 1
            split_ahead(i + ahead)
            return i % SPLIT, (high[i], low_parts[i])

        PASSES = ((0, 0), (1, 0), (0, 1))

        def rows_piece(operand, i, t, kh, bk):
            if kh == 0:
                wait_bank(bk)
            for n in range(KPIECE):
                k = kh * KPIECE + n
                pe.wait(*operand.when(k, i))
                for m, (a, w) in enumerate(PASSES):
                    first, last = k == 0 and m == 0, k == KT - 1 and m == 2
                    step = (lambda e, k=k, a=a, w=w, n=n, first=first, last=last:
                            e.matmul(bank[bk][:], (operand.hi, operand.lo)[a][:, k, i * P:(i + 1) * P],
                                     (w_hi, w_lo)[w][:, t, n], start=first, stop=last))
                    if n == KPIECE - 1 and m == 2:
                        return pe.do(step)
                    pe.run(step)

        def product_rows(operand, evacuate, banks):
            for kh in range(2):
                t, ready = next_piece(SPLIT)
                pe.wait(*ready)
                for i in range(NT):
                    done = rows_piece(operand, i, t, kh, banks[i])
                    if kh == 1:
                        read_by(banks[i], evacuate(i, banks[i], done))
                split_free[t] = [done]

        next_bank = [0]

        def product_cols(operand, c, evacuate):
            ring = (3, 4, 5, 6, 7)
            banks = [ring[(next_bank[0] + m) % 5] for m in range(4)]
            next_bank[0] += 4
            for kh in range(2):
                t, ready = next_piece(SPLIT)
                pe.wait(*ready)
                for f in range(HALF // P):
                    bk = banks[f]
                    if kh == 0:
                        wait_bank(bk)
                    for n in range(KPIECE):
                        k = kh * KPIECE + n
                        pe.wait(*(when for i in range(NT) for when in operand.when(k, i)))
                        for m, (a, w) in enumerate(PASSES):
                            first, last = k == 0 and m == 0, k == KT - 1 and m == 2
                            step = (lambda e, bk=bk, k=k, f=f, a=a, w=w, n=n, t=t, first=first, last=last:
                                    e.matmul(bank[bk][:, 0:N], (w_hi, w_lo)[w][:, t, n, f * P:(f + 1) * P],
                                             (operand.hi, operand.lo)[a][:, k, :], start=first, stop=last))
                            if n == KPIECE - 1 and m == 2:
                                done = pe.do(step)
                            else:
                                pe.run(step)
                    if kh == 1:
                        read_by(bk, evacuate(c * (HALF // P) + f, bk, done))
                split_free[t] = [done]
                yield

        x_tiles = A["x"].rearrange("(t p) d -> p t d", p=P)
        got_x = [Arrival(sem(f"x_in{i}")).load(sync, x_rows[:, i], x_tiles[:, i]) for i in range(NT)]
        load_ahead(RAW)
        small = Arrival(sem("small_in"))
        for i, name in enumerate(("bq", "biq", "bk", "bik", "bv")):
            small.load(sync, cols[:, i, :], A[name])
        for i, name in enumerate(("src_cols", "dst_cols", "type_cols")):
            small.load(sync, ecol_i[:, i, :], A[name])
        small.load(sync, router_raw[:], A["router"].rearrange("(k p) e -> p k e", p=P))
        small.load(sync, e_bias[:], A["e_bias"].partition_broadcast(P))
        got_small = small.load(sync, etw[:, 0, :], A["etw"].partition_broadcast(P))

        row_in = Arrival(sem("edge_rows_in"))
        bias_in = Arrival(sem("bias_in"))

        pool.do(lambda e: e.memset(ident[:], 0.0))
        have_half = pool.do(lambda e: e.memset(half_neg[:], -0.5))
        pool.chain(lambda e: e.memset(diag[:], 0.0))
        have_ident = pool.do(lambda e: e.affine_select(out=ident[:], in_=ident[:], compare_op=ALU.not_equal,
                                                       fill=1.0, base=0, pattern=[[-1, P]],
                                                       channel_multiplier=1))
        have_diag = pool.do(lambda e: e.affine_select(out=diag[:], in_=diag[:], compare_op=ALU.not_equal,
                                                      fill=0.5, base=0, pattern=[[P, NT], [-1, N]],
                                                      channel_multiplier=1))
        have_node = pool.do(lambda e: e.iota(node[:], pattern=[[1, N]], base=0, channel_multiplier=0,
                                             allow_small_or_imprecise_dtypes=True))
        pool.chain(lambda e: e.memset(later[:], 1.0))
        have_later = pool.do(lambda e: e.affine_select(out=later[:], in_=later[:], compare_op=ALU.is_gt,
                                                       fill=0.0, base=0, pattern=[[1, SUPER * P]],
                                                       channel_multiplier=-1))

        def half_stats(i, hh):
            return dve.do(lambda e: e.bn_stats(stats[:, i, hh, :], x_rows[:, i, hh * HALF:(hh + 1) * HALF]))

        def norm_scale(i, stat):
            dve.wait(stat)
            dve.chain(lambda e: e.bn_aggr(meanvar[:, i, :], stats[:, i].rearrange("p a b -> p (a b)")))
            var = dve.do(lambda e: e.tensor_scalar(rstd[:, i:i + 1], meanvar[:, i, 1:2], EPS, None, ALU.add))
            pool.wait(var, have_half)
            return pool.do(lambda e: e.tensor_tensor(rstd[:, i:i + 1], rstd[:, i:i + 1], half_neg[:, 0:1],
                                                     ALU.pow))

        def norm_apply(target, i, scale):
            dve.wait(scale)
            return dve.do(lambda e: e.tensor_scalar(target[:, i, :], x_rows[:, i, :], meanvar[:, i, 0:1],
                                                    rstd[:, i:i + 1], ALU.subtract, ALU.mult))

        def split_out(bk, source, hi, lo, ready, bias=None):
            act.wait(ready)
            if bias is None:
                h = act.do(lambda e: e.activation(hi, source, ACT.Copy))
                dve.wait(h)
                done = dve.do(lambda e: e.tensor_tensor(lo, source, hi.bitcast(F32), ALU.subtract))
            else:
                h = act.do(lambda e: e.activation(hi, source, ACT.Identity, bias=bias))
                dve.wait(h)
                done = dve.do(lambda e: e.scalar_tensor_tensor(lo, source, bias, hi.bitcast(F32),
                                                               ALU.add, ALU.subtract))
            read_by(bk, done)
            return done

        def turn(source, operand, b, t, bk, *ready):
            pe.wait(have_ident, *ready)
            wait_bank(bk)
            for m in range(HALF // P):
                step = (lambda e, m=m: e.transpose(bank[bk][:, m * P:(m + 1) * P],
                                                   source[:, m * P:(m + 1) * P], ident[:]))
                if m == HALF // P - 1:
                    done = pe.do(step)
                else:
                    pe.run(step)
            ks, ts = slice(4 * b, 4 * b + 4), slice(t * P, (t + 1) * P)
            got = split_out(bk, bank[bk][:].rearrange("p (k n) -> p k n", n=P),
                            operand.hi[:, ks, ts], operand.lo[:, ks, ts], done)
            for k in range(4 * b, 4 * b + 4):
                operand.ready[k, t] = got
            return done

        def edge_weights():
            dve.wait(got_small)
            act.wait(got_small)
            dve.chain(lambda e: e.tensor_scalar(etw[:, 1, :], etw[:, 0, :], -1.0, None, ALU.mult))
            d = dve.chain(lambda e: e.tensor_tensor(etw[:, 1, :], etw[:, 1, :], etw[:, 0, :], ALU.min))
            act.wait(d)
            act.chain(lambda e: e.activation(etw[:, 2, :], etw[:, 1, :], ACT.Exp))
            a = act.do(lambda e: e.activation(etw[:, 3, :], etw[:, 2, :], ACT.Ln, bias=1.0))
            dve.chain(lambda e: e.tensor_scalar(etw[:, 4, :], etw[:, 0, :], 0.0, None, ALU.max))
            dve.wait(a)
            dve.chain(lambda e: e.tensor_tensor(etw[:, 4, :], etw[:, 4, :], etw[:, 3, :], ALU.add))
            dve.chain(lambda e: e.tensor_scalar(etw[:, 5, :], etw[:, 4, :], 8.0, None, ALU.mult))

        def edge_values():
            for i in range(3):
                last = dve.do(lambda e, i=i: e.tensor_copy(ecol[:, i, :], ecol_i[:, i, :]))
            for s in range(NS):
                last = dve.do(lambda e, s=s: e.memset(ecol[:, 6, s * SUPER:(s + 1) * SUPER], float(16 ** s)))
            dve.wait(last)
            have_ecol.append(last)
            dve.do(lambda e: e.scalar_tensor_tensor(ecol[:, 3, :], ecol[:, 0, :], float(N), ecol[:, 1, :],
                                                    ALU.mult, ALU.add))
            dve.chain(lambda e: e.tensor_scalar(ecol[:, 4, :], ecol[:, 2, :], 1.0, 1.0, ALU.is_equal, ALU.mult))
            for kind, code in ((2, 2.0), (3, 4.0), (4, 8.0), (0, 8.0)):
                dve.chain(lambda e, kind=kind, code=code: e.tensor_scalar(
                    ecol[:, 5, :], ecol[:, 2, :], float(kind), code, ALU.is_equal, ALU.mult))
                dve.chain(lambda e: e.tensor_tensor(ecol[:, 4, :], ecol[:, 4, :], ecol[:, 5, :], ALU.add))
            dve.chain(lambda e: e.tensor_tensor(ecol[:, 4, :], ecol[:, 4, :], ecol[:, 6, :], ALU.mult))

        edge_state, have_ecol = {}, []

        def load_edge_rows(s):
            if "rows_read" in edge_state:
                pool.wait(edge_state["rows_read"])
            row_in.load(pool, src_row, A["src"][s * SUPER * P:(s + 1) * SUPER * P].partition_broadcast(P))
            edge_state["rows"] = row_in.load(
                pool, dst_row, A["dst"][s * SUPER * P:(s + 1) * SUPER * P].partition_broadcast(P))

        def edge_keys(s):
            dve.wait(edge_state["rows"], have_later)
            edge_state["rows_read"] = dve.chain(lambda e: e.scalar_tensor_tensor(
                key_row, src_row, float(N), dst_row, ALU.mult, ALU.add))

        def edge_twins(s, j):
            c, width = s * SUPER + j, (SUPER - j) * P
            dve.chain(lambda e: e.scalar_tensor_tensor(
                same[:, 0:width], key_row[:, j * P:], ecol[:, 3, c:c + 1], later[:, 0:width],
                ALU.is_equal, ALU.mult, accum_out=ecol[:, 7, c:c + 1]))
            if j == SUPER // 2 and s + 1 < NS:
                load_edge_rows(s + 1)
            if j == SUPER - 1:
                cut = slice(s * SUPER, (s + 1) * SUPER)
                dve.chain(lambda e: e.scalar_tensor_tensor(ecol[:, 4, cut], ecol[:, 7, cut], 0.0,
                                                           ecol[:, 4, cut], ALU.is_equal, ALU.mult))

        edge_products = []

        def edge_chunk(c):
            o = c % ONEHOTS
            while len(edge_products) >= ONEHOTS:
                edge_products.pop(0)()
            if c >= ONEHOTS:
                dve.wait(edge_state[c - ONEHOTS])
                pool.wait(edge_state[c - ONEHOTS])
            dve.wait(have_node)
            pool.wait(have_ecol[0])
            hot_src = pool.do(lambda e: e.tensor_scalar(onehot_src[:, o], node[:], ecol[:, 0, c:c + 1], None,
                                                        ALU.is_equal))
            hot = dve.do(lambda e: e.tensor_scalar(onehot_dst[:, o], node[:], ecol[:, 1, c:c + 1],
                                                   ecol[:, 4, c:c + 1], ALU.is_equal, ALU.mult))

            def products():
                pe.wait(hot, hot_src)
                for i in range(NT):
                    done = pe.do(lambda e, i=i: e.matmul(bank[i][:, 0:N], onehot_src[:, o, i * P:(i + 1) * P],
                                                         onehot_dst[:, o], start=(c == 0), stop=(c == EC - 1)))
                edge_state[c] = done
            edge_products.append(products)

        def edge_mask():
            while edge_products:
                edge_products.pop(0)()
            digits = k2_flat[:, 0:NT * N].rearrange("p (t n) -> p t n", t=NT)
            kind = k2_flat[:, NT * N:2 * NT * N].rearrange("p (t n) -> p t n", t=NT)
            dve.wait(edge_state[EC - 1], have_diag)
            for i in range(NT):
                last = dve.do(lambda e, i=i: e.tensor_tensor(digits[:, i], bank[i][:, 0:N], diag[:, i], ALU.max))
                read_by(i, last)
            dve.wait(last)
            dve.do(lambda e: e.tensor_scalar(mask8[:], digits, 0.0, 8.0 * ABSENT, ALU.is_equal, ALU.mult))
            dve.chain(lambda e: e.tensor_scalar(kind.bitcast(I32), digits.bitcast(I32), 23, 3,
                                                ALU.logical_shift_right, ALU.bitwise_and))
            for w, code in enumerate((3.0, 0.0, 1.0, 2.0)):
                dve.chain(lambda e, w=w, code=code: e.tensor_scalar(
                    digits, kind.bitcast(I32), code, etw[:, 5, w:w + 1], ALU.is_equal, ALU.mult))
                last = dve.chain(lambda e: e.tensor_tensor(mask8[:], mask8[:], digits, ALU.add))
            return last

        x_in, mid = Operand(in_hi, in_lo), Operand(mid_hi, mid_lo)
        normed = []
        act.wait(have_half)
        act.do(lambda e: e.activation(warm[:], half_neg[:], ACT.Copy))
        def keep_busy(n):
            pe.wait(have_ident)
            for _ in range(n):
                pe.run(lambda e: e.transpose(bank[0][:, 0:P], ident[:], ident[:]))

        scale = []
        for i in range(NT):
            dve.wait(got_x[i])
            half_stats(i, 0)
            scale.append(norm_scale(i, half_stats(i, 1)))
            if i:
                normed.append(norm_apply(rows, i - 1, scale[i - 1]))
        for i in range(NT):
            keep_busy((22, 4, 8)[i])
            if i == NT - 1:
                normed.append(norm_apply(rows, i, scale[i]))
                split_ahead(1)
            for b in range(2):
                turn(rows[:, i, b * HALF:(b + 1) * HALF], x_in, b, i, 3 + (2 * i + b) % 5, normed[i])
        keep_busy(8)
        load_edge_rows(0)

        def to_mid(col):
            def evacuate(k, bk, done):
                mid.ready[k] = split_out(bk, bank[bk][:, 0:N], mid_hi[:, k, :], mid_lo[:, k, :], done,
                                         bias=cols[:, col, k:k + 1])
                return mid.ready[k]
            return evacuate

        def to_plain(target, col):
            def evacuate(k, bk, done):
                act.wait(done)
                return act.do(lambda e: e.activation(target[:, k, :], bank[bk][:, 0:N], ACT.Identity,
                                                     bias=cols[:, col, k:k + 1]))
            return evacuate

        edge_work = [edge_weights, edge_values]
        for s in range(NS + 1):
            if s < NS:
                edge_work.append(lambda s=s: edge_keys(s))
            for j in range(SUPER):
                if s < NS:
                    edge_work.append(lambda s=s, j=j: edge_twins(s, j))
                if s > 0:
                    edge_work.append(lambda c=(s - 1) * SUPER + j: edge_chunk(c))
        PROJECTIONS = ((x_in, to_mid(0)), (mid, to_plain(q2, 1)), (x_in, to_mid(2)), (x_in, None),
                       (mid, to_plain(k2, 3)), (x_in, to_mid(4)))
        SHADOW = 12
        share = -(-len(edge_work) // (SHADOW - 1))

        def between():
            while edge_products:
                edge_products.pop(0)()
            for _ in range(share if taken[0] > 1 else 1):
                if edge_work:
                    edge_work.pop(0)()

        act.wait(got_small)
        hi = act.do(lambda e: e.activation(router_hi[:], router_raw[:], ACT.Copy))
        dve.wait(hi, got_small)
        have_router = dve.do(lambda e: e.tensor_tensor(router_lo[:], router_raw[:], router_hi[:].bitcast(F32),
                                                       ALU.subtract))
        have_mask = None
        for operand, evacuate in PROJECTIONS:
            if evacuate is None:
                while edge_work:
                    edge_work.pop(0)()
                have_mask = edge_mask()
                act.wait(have_mask)
                sync.wait(have_mask)
                biv_in = bias_in.load(sync, row_bias[:], A["biv"].partition_broadcast(P))
                continue
            for c in range(2):
                for _ in product_cols(operand, c, evacuate):
                    between()

        def to_v2(c):
            def evacuate(i, bk, done):
                dve.wait(done, biv_in)
                return dve.do(lambda e: e.tensor_tensor(v2[:, i, c * HALF:(c + 1) * HALF], bank[bk][:],
                                                        row_bias[:, c * HALF:(c + 1) * HALF], ALU.add))
            return evacuate

        have_k2 = (act.sems[0], act.counts[0])
        heads = [(i, h) for i in range(NT) for h in range(HEADS)]
        token = {}

        def scores(n):
            i, h = heads[n]
            base, k = (h % 2) * DH, h // 2
            bk = n % 3
            wait_bank(bk)
            pe.wait(have_k2)
            token["s", n] = pe.do(lambda e: e.matmul(bank[bk][:, 0:N], q2[base:base + DH, k, i * P:(i + 1) * P],
                                                     k2[base:base + DH, k, :], start=True, stop=True))

        def softmax(n):
            i, h = heads[n]
            bk, o, q, pb = n % 3, n % 2, n % 4, n % 4
            if n >= 2:
                dve.wait(token["e", n - 2])
            dve.wait(token["s", n], have_mask)
            m = dve.do(lambda e: e.tensor_tensor_reduce(
                out=score[:, o], in0=bank[bk][:, 0:N], in1=mask8[:, i],
                scale=-1.0 / 8.0, scalar=3.0e38, op0=ALU.add, op1=ALU.min, accum_out=low[:, q:q + 1]))
            read_by(bk, m)
            act.wait(m)
            if n >= 4:
                act.wait(token["t", n - 4])
            if i >= 2:
                act.wait(token["inverse", i - 2, h // 8])
            token["e", n] = act.do(lambda e: e.activation(prob[:, pb], score[:, o], ACT.Exp, scale=-1.0,
                                                          bias=low[:, q:q + 1],
                                                          accum_out=sums[:, i % 2, h:h + 1]))

        def turn_probabilities(n):
            bk, o = 3 + n % 2, n % 4
            wait_bank(bk)
            pe.wait(token["e", n])
            for m in range(NT):
                step = (lambda e, m=m: e.transpose(bank[bk][:, m * P:(m + 1) * P],
                                                   prob[:, o, m * P:(m + 1) * P], ident[:]))
                done = pe.do(step)
            token["t", n] = done
            act.wait(done)
            if n >= 2:
                act.wait(token["o", n - 2])
            token["c", n] = act.do(lambda e: e.activation(
                prob_t[:, n % 2], bank[bk][:, 0:N].rearrange("p (m n) -> p m n", m=NT), ACT.Copy))
            read_by(bk, token["c", n])

        def attend(n):
            i, h = heads[n]
            b, at = h // 8, (h % 8) * DH
            bk = 5 + b
            if at == 0:
                wait_bank(bk)
            pe.wait(token["c", n], have_v2)
            for m in range(NT):
                done = pe.do(lambda e, m=m: e.matmul(bank[bk][:, at:at + DH], prob_t[:, n % 2, m, :],
                                                     v2[:, m, h * DH:(h + 1) * DH], start=(m == 0),
                                                     stop=(m == NT - 1)))
            token["o", n] = done
            if h % 8 == 7:
                cut = sums[:, i % 2, b * 8:(b + 1) * 8]
                dve.wait(token["e", n])
                inverse = token["inverse", i, b] = dve.do(lambda e: e.reciprocal(cut, cut))
                dve.wait(inverse, done)
                if i:
                    dve.wait(token["turned", b])
                token["attended", b] = dve.do(lambda e: e.tensor_tensor(
                    attended[:, b].rearrange("p (h d) -> p h d", d=DH),
                    bank[bk][:].rearrange("p (h d) -> p h d", d=DH),
                    cut.unsqueeze(2).to_broadcast([P, 8, DH]), ALU.mult))
                read_by(bk, token["attended", b])
                to_turn.append((n + AHEAD + 3, lambda: token.update({("turned", b): turn(
                    attended[:, b], x_in, b, i, 7, token["attended", b])})))

        to_turn = []
        AHEAD = 3
        for n in range(len(heads) + AHEAD + 1):
            if n < AHEAD - 1:
                product_rows(mid, to_v2(n), (5, 6, 7) if n else (3, 4, 5))
            if n < len(heads):
                scores(n)
            if n >= AHEAD and n - AHEAD < len(heads):
                turn_probabilities(n - AHEAD)
            if n == AHEAD - 1:
                have_v2 = (dve.sems[0], dve.counts[0])
            if n > AHEAD:
                attend(n - AHEAD - 1)
            if n < len(heads):
                softmax(n)
            while to_turn and to_turn[0][0] <= n:
                to_turn.pop(0)[1]()
        while to_turn:
            to_turn.pop(0)[1]()

        pool.wait(token["s", len(heads) - 1])
        bo_in = Arrival(sem("bo_in")).load(pool, row_bias[:], A["bo"].partition_broadcast(P))
        got_x = Arrival(sem("x_again_in")).load(pool, x_again, x_tiles)

        dve.wait(bo_in, got_x)
        for i in range(NT):
            for c in range(2):
                biased_x = dve.do(lambda e, i=i, cut=slice(c * HALF, (c + 1) * HALF): e.tensor_tensor(
                    x_again[:, i, cut], x_again[:, i, cut], row_bias[:, cut], ALU.add))

        def to_residual(c):
            cut = slice(c * HALF, (c + 1) * HALF)

            def evacuate(i, bk, done):
                dve.wait(done, biased_x)
                token["x", i, c] = dve.chain(lambda e: e.tensor_tensor(x_rows[:, i, cut], bank[bk][:],
                                                                      x_again[:, i, cut], ALU.add))
                stat = half_stats(i, c)
                if c:
                    token["scale", i] = norm_scale(i, stat)
                    if i:
                        token["normed", i - 1] = norm_apply(rows2, i - 1, token["scale", i - 1])
                return token["x", i, c]
            return evacuate

        for c in range(2):
            product_rows(x_in, to_residual(c), (0, 1, 2) if c else (3, 4, 7))


        def turn_x(t, banks, *ready):
            for b in range(2):
                token["turned x", t] = turn(rows2[:, t, b * HALF:(b + 1) * HALF], x_in, b, t, banks[b], *ready)

        turn_x(0, (6, 7), token["normed", 0])
        token["normed", NT - 1] = norm_apply(rows2, NT - 1, token["scale", NT - 1])
        turn_x(1, (6, 0), token["normed", 1])

        graph_over = [token["x", NT - 1, 1], token["inverse", NT - 1, 1]]

        pool.wait(*(token["normed", i] for i in range(NT)))
        rows_out = Arrival(sem("rows_out"))
        rows_out.load(pool, normed_dram.rearrange("(t p) d -> p t d", p=P), rows2[:])
        have_normed = rows_out.load(pool, out[N:N + P, :], rows2[:, 0, :])

        pool.do(lambda e: e.memset(ones16[:], 1.0))
        pool.do(lambda e: e.memset(before[:], 1.0))
        pool.chain(lambda e: e.memset(earlier[:], 1.0))
        pool.do(lambda e: e.affine_select(
            out=earlier[:], in_=earlier[:], compare_op=ALU.is_gt, fill=0.0, base=0,
            pattern=[[1, EXPERTS], [-1, EXPERTS]], channel_multiplier=0))
        pool.do(lambda e: e.affine_select(out=before[:], in_=before[:], compare_op=ALU.is_gt, fill=0.0, base=0,
                                          pattern=[[1, P]], channel_multiplier=-1))
        pool.do(lambda e: e.iota(slot[:], pattern=[[1, N]], base=0, channel_multiplier=0,
                                 allow_small_or_imprecise_dtypes=True))
        pool.do(lambda e: e.iota(tile_start[:], pattern=[[P, NT]], base=0, channel_multiplier=0,
                                 allow_small_or_imprecise_dtypes=True))
        pool.do(lambda e: e.iota(row_in_tile[:], pattern=[[0, NT]], base=0, channel_multiplier=1,
                                 allow_small_or_imprecise_dtypes=True))
        have_tables = pool.do(lambda e: e.iota(spare_row[:, 0:1], pattern=[[0, 1]], base=N, channel_multiplier=1,
                                               allow_small_or_imprecise_dtypes=True))

        biased, masked, chosen, tmp = r
        four = biased[:].rearrange("p t (g s) -> p t g s", s=GSIZE)

        def router():
            wait_bank(2)
            pe.wait(have_router)
            for i in range(NT):
                for k in range(KT):
                    pe.wait(*x_in.when(k, i))
                    for m, (a, w) in enumerate(PASSES):
                        step = (lambda e, i=i, k=k, m=m, a=a, w=w: e.matmul(
                            bank[2][:, i * EXPERTS:(i + 1) * EXPERTS],
                            (x_in.hi, x_in.lo)[a][:, k, i * P:(i + 1) * P],
                            (router_hi, router_lo)[w][:, k, :], start=(k == 0 and m == 0),
                            stop=(k == KT - 1 and m == 2)))
                        if k == KT - 1 and m == 2:
                            done = pe.do(step)
                        else:
                            pe.run(step)
            act.wait(done)
            token["sig"] = act.do(lambda e: e.activation(
                prob_e[:], bank[2][:, 0:NT * EXPERTS].rearrange("p (t e) -> p t e", t=NT), ACT.Sigmoid))
            read_by(2, token["sig"])

        def group_scores():
            dve.wait(token["sig"], have_tables)
            for i in range(NT):
                last = dve.do(lambda e, i=i: e.tensor_tensor(biased[:, i], prob_e[:, i], e_bias[:], ALU.add))
            dve.wait(last)
            a_, b_, c_, d_ = (four[:, :, :, j] for j in range(GSIZE))
            dve.do(lambda e: e.tensor_tensor(gs[:, :, 0], a_, b_, ALU.max))
            dve.do(lambda e: e.tensor_tensor(gs[:, :, 1], a_, b_, ALU.min))
            dve.do(lambda e: e.tensor_tensor(gs[:, :, 2], c_, d_, ALU.max))
            dve.chain(lambda e: e.tensor_tensor(gs[:, :, 3], c_, d_, ALU.min))
            dve.do(lambda e: e.tensor_tensor(gs[:, :, 4], gs[:, :, 0], gs[:, :, 2], ALU.max))
            dve.do(lambda e: e.tensor_tensor(gs[:, :, 5], gs[:, :, 0], gs[:, :, 2], ALU.min))
            dve.chain(lambda e: e.tensor_tensor(gs[:, :, 1], gs[:, :, 1], gs[:, :, 3], ALU.max))
            dve.chain(lambda e: e.tensor_tensor(gs[:, :, 5], gs[:, :, 5], gs[:, :, 1], ALU.max))
            dve.chain(lambda e: e.tensor_tensor(gs[:, :, 0], gs[:, :, 4], gs[:, :, 5], ALU.add))

        def rank_of(values, n, result):
            rival = values.unsqueeze(1).to_broadcast([P, n, n])
            own = values.unsqueeze(2).to_broadcast([P, n, n])
            bb, b2 = beats[:, 0:n, 0:n], beats2[:, 0:n, 0:n]
            dve.do(lambda e: e.tensor_tensor(bb, rival, own, ALU.is_gt))
            dve.chain(lambda e: e.tensor_tensor(b2, rival, own, ALU.is_equal))
            dve.chain(lambda e: e.tensor_tensor(b2, b2, earlier[:, 0:n, 0:n], ALU.mult))
            dve.chain(lambda e: e.tensor_tensor(bb, bb, b2, ALU.add))
            dve.chain(lambda e: e.tensor_reduce(result, bb, AX.X, ALU.add))

        def mask_groups():
            dve.chain(lambda e: e.tensor_scalar(gs[:, :, 2], gs[:, :, 1], 1.5, None, ALU.is_lt))
            dve.chain(lambda e: e.tensor_scalar(gs[:, :, 3], gs[:, :, 2], -1.0, None, ALU.add))
            for i in range(NT):
                inside = gs[:, i, 2].unsqueeze(2).to_broadcast([P, GROUPS, GSIZE])
                less = gs[:, i, 3].unsqueeze(2).to_broadcast([P, GROUPS, GSIZE])
                grouped = masked[:, i].rearrange("p (g s) -> p g s", s=GSIZE)
                dve.chain(lambda e, i=i, inside=inside, grouped=grouped: e.tensor_tensor(
                    grouped, four[:, i], inside, ALU.mult))
                dve.chain(lambda e, less=less, grouped=grouped: e.tensor_tensor(grouped, grouped, less, ALU.add))

        def weigh():
            dve.chain(lambda e: e.tensor_scalar(chosen[:], tmp[:], GSIZE - 0.5, None, ALU.is_lt))
            token["chosen"] = dve.do(lambda e: e.tensor_copy(chosen16[:], chosen[:]))
            dve.chain(lambda e: e.tensor_tensor(tmp[:], chosen[:], prob_e[:], ALU.mult))
            dve.chain(lambda e: e.tensor_reduce(denom[:], tmp[:], AX.X, ALU.add))
            dve.chain(lambda e: e.tensor_scalar(denom[:], denom[:], 1e-20, None, ALU.add))
            dve.chain(lambda e: e.reciprocal(denom[:], denom[:]))
            for i in range(NT):
                last = dve.do(lambda e, i=i: e.tensor_scalar(combine[:, i], tmp[:, i], denom[:, i:i + 1],
                                                             ROUTE_SCALE, ALU.mult, ALU.mult))
            dve.wait(last)

        def place_tokens():
            pe.wait(token["chosen"], have_tables)
            wait_bank(6)
            for i in range(NT + 1):
                terms = [(ones16, j) for j in range(min(i, NT))] + ([(before, i)] if i < NT else [])
                for n, (lhs, j) in enumerate(terms):
                    done = pe.do(lambda e, i=i, lhs=lhs, j=j, n=n, last=len(terms) - 1: e.matmul(
                        bank[6][:, i * EXPERTS:(i + 1) * EXPERTS], lhs[:], chosen16[:, j],
                        start=(n == 0), stop=(n == last)))
            token["placed"] = done

        def use_places():
            dve.wait(token["placed"])
            got = dve.do(lambda e: e.tensor_copy(
                place[:], bank[6][:, 0:(NT + 1) * EXPERTS].rearrange("p (t e) -> p t e", e=EXPERTS)))
            read_by(6, got)
            dve.wait(got)
            for x in range(EXPERTS):
                dve.do(lambda e, x=x: e.memset(bits[:, :, x:x + 1], float(2 ** x)))
            for t in range(1, NT):
                dve.do(lambda e, t=t: e.tensor_scalar(more[:, t - 1], place[:, NT], float(t * P), None, ALU.is_gt))
            dve.wait((dve.sems[0], dve.counts[0]))
            dve.chain(lambda e: e.tensor_tensor(more[:], more[:], bits[:], ALU.mult))
            dve.chain(lambda e: e.tensor_reduce(words_f[:], more[:], AX.X, ALU.add))
            token["words"] = dve.do(lambda e: e.tensor_copy(words[:], words_f[:]))
            dve.do(lambda e: e.tensor_scalar(spare_row[:, 1:2], spare_row[:, 0:1], -1.0, None, ALU.mult))
            dve.chain(lambda e: e.tensor_tensor(place[:, 0:NT], place[:, 0:NT], chosen[:], ALU.mult))
            dve.chain(lambda e: e.tensor_tensor(place[:, 0:NT], place[:, 0:NT], chosen[:], ALU.add))
            dve.chain(lambda e: e.tensor_scalar(place[:, 0:NT], place[:, 0:NT], -1.0, None, ALU.add))
            for n, values in enumerate((tile_start, row_in_tile)):
                dve.do(lambda e, n=n, values=values: e.tensor_copy(
                    info[:, :, :, n], values[:].unsqueeze(2).to_broadcast([P, NT, EXPERTS])))
            dve.do(lambda e: e.tensor_scalar(info[:, :, :, 2], combine[:], 0.0, 1.0, ALU.mult, ALU.add))
            dve.chain(lambda e: e.tensor_copy(info[:, :, :, 3], combine[:]))
            dve.chain(lambda e: e.tensor_tensor(weight_rest[:], combine[:], info[:, :, :, 3], ALU.subtract))
            dve.chain(lambda e: e.tensor_copy(info[:, :, :, 4], weight_rest[:]))
            dve.chain(lambda e: e.tensor_tensor(weight_rest[:], weight_rest[:], info[:, :, :, 4], ALU.subtract))
            dve.do(lambda e: e.tensor_copy(info[:, :, :, 5], weight_rest[:]))

        def choose(first):
            if first:
                dve.wait(token["slots", first - 1])
            for x in (first, first + 1):
                for i in range(NT):
                    token["chooses"] = dve.do(lambda e, x=x, i=i: e.tensor_scalar(
                        chooses[:, x % 2, i], slot[:], place[:, i, x:x + 1], None, ALU.is_equal))

        def find_slots(first):
            pe.wait(token["chooses"])
            wait_bank(7)
            for x in (first, first + 1):
                for j in range(NT):
                    n = (x % 2 * NT + j) * FACTS
                    for i in range(NT):
                        done = pe.do(lambda e, x=x, i=i, j=j, n=n: e.matmul(
                            bank[7][:, n:n + FACTS], chooses[:, x % 2, i, j * P:(j + 1) * P], info[:, i, x, :],
                            start=(i == 0), stop=(i == NT - 1)))
            token["slots", x] = done
            dve.wait(done)
            got = dve.chain(lambda e: e.tensor_copy(
                slots[:, first * NT:(first + 2) * NT],
                bank[7][:, 0:2 * NT * FACTS].rearrange("p (s c) -> p s c", c=FACTS)))
            read_by(7, got)

        def slot_tables(first):
            at = slice(first * NT, (first + 2) * NT)
            dve.chain(lambda e: e.tensor_tensor(slot_from[:, at], slots[:, at, 0], slots[:, at, 1], ALU.add))
            dve.do(lambda e: e.tensor_copy(gather_at[:, at], slot_from[:, at]))
            dve.do(lambda e: e.tensor_tensor(slot_w[:, at], slots[:, at, 3], slots[:, at, 4], ALU.add))
            dve.chain(lambda e: e.tensor_scalar(slot_to[:, at], slots[:, at, 2], spare_row[:, 1:2],
                                                spare_row[:, 0:1], ALU.mult, ALU.add))
            dve.do(lambda e: e.tensor_tensor(slot_w[:, at], slot_w[:, at], slots[:, at, 5], ALU.add))
            dve.chain(lambda e: e.tensor_tensor(slot_to[:, at], slot_to[:, at], slot_from[:, at], ALU.add))
            tables = dve.do(lambda e: e.tensor_copy(scatter_at[:, at], slot_to[:, at]))
            token["tables", first] = token["tables", first + 1] = tables

        def routing():
            router()
            group_scores()
            for i in range(NT):
                rank_of(gs[:, i, 0], GROUPS, gs[:, i, 1])
            mask_groups()
            for i in range(NT):
                rank_of(masked[:, i], EXPERTS, tmp[:, i])
            weigh()

        def placing():
            place_tokens()
            use_places()
            choose(0)

        def slotting(first):
            find_slots(first)
            if first + 2 < EXPERTS:
                choose(first + 2)
            slot_tables(first)

        side = [routing, placing] + [lambda x=x: slotting(x) for x in range(0, EXPERTS, 2)]

        registers = {}

        def load_words():
            for lane in (pe, act, dve, pool):
                lane.wait(token["words"])

                def load(e, lane=lane):
                    registers[id(lane)] = [e.value_load(words[0:1, t:t + 1], min_val=0, max_val=2 ** EXPERTS - 1)
                                           for t in range(NT - 1)]
                lane.run(load)

        gathered = [Arrival(sem(f"gathered{t}")) for t in range(NT)]
        scattered = [Arrival(sem(f"scattered{t}")) for t in range(NT)]

        indirect = (*gathered, *scattered)

        @contextmanager
        def section(x, t):
            lanes = (pe, act, dve, pool)
            kept = [(lane.steps, lane.track, dict(lane.waited), list(lane.counts)) for lane in lanes]
            arrivals = [a.count for a in indirect]
            for lane in lanes:
                lane.steps, lane.track = [], t
            yield
            for lane, (steps, track, waited, counts_before) in zip(lanes, kept):
                body, lane.steps, lane.track, lane.waited = lane.steps, steps, track, waited
                if not body:
                    continue
                missing = [(s_, was, now - was)
                           for s_, was, now in zip(lane.sems, counts_before, lane.counts) if now > was]
                unsent = [(a.sem, was, n) for n, (a, was) in enumerate(zip(indirect, arrivals))
                          if lane is pool and a.count > was]

                def branch(e, lane=lane, body=body, missing=missing, unsent=unsent):
                    with e.If((registers[id(lane)][t - 1] & 2 ** x) > 0):
                        for step in body:
                            step(e)
                    with e.Else():
                        for s_, was, n in missing:
                            if was:
                                e.wait_ge(s_, was)
                            e.sem_inc(s_, n)
                        for s_, was, n in unsent:
                            if was:
                                e.wait_ge(s_, was)
                            e.dma_start(idle[:, n:n + 1], ident[0:1, 0:1]).then_inc(s_, 16)
                lane.run(branch)

        def each_tile(u, work, first=0):
            if first == 0:
                work(0)
            if u < SHARED:
                work(1)
                work(2)
            else:
                with section(u - SHARED, 1):
                    work(1)
                    with section(u - SHARED, 2):
                        work(2)

        def gather(x, t):
            n = x * NT + t
            pool.wait(token["tables", x], have_normed)
            if ("turned x", t) in token:
                pool.wait(token["turned x", t])
            token["gathered", t] = gathered[t].start(pool, lambda e: e.indirect_dma_start(
                out=rows2[:, t, :], out_offset=None, in_=normed_dram,
                in_offset=bass.IndirectOffsetOnAxis(ap=gather_at[:, n:n + 1], axis=0)))

        hid = Operand(act_hi, act_lo)

        def turn_hidden(c, t):
            token["hidden turned", t] = turn(hidden[:, t], hid, c, t, 6 + (t + c) % 2, token["hidden", t])

        GATE_BANK, UP_BANK = (0, 4, 5), (1, 4, 5)
        DOWN_BANKS = ((2, 3), (4, 5), (0, 1))

        def stage(u, s):
            (t0, ready0), (t1, ready1) = next_piece(), next_piece()
            split_high(taken[0] + 2)
            split_low(taken[0] + 1)
            pe.wait(*ready0)
            c = s // 2

            follows = u + 1 >= SHARED and u + 1 < UNITS

            def turn_next(t):
                turn_x(t, (6, 7) if t else (6, 0), token["gathered", t])

            def tile(t):
                if u == 0 and s == 0 and t == 1:
                    turn_x(NT - 1, (6, 7), token["normed", NT - 1])
                if s < 4:
                    bk = (GATE_BANK, UP_BANK)[s % 2][t]
                    rows_piece(x_in, t, t0, 0, bk)
                    if t == 0:
                        pe.wait(*ready1)
                    done = rows_piece(x_in, t, t1, 1, bk)
                    if s % 2 == 0:
                        act.wait(done)
                        if ("hidden", t) in token:
                            act.wait(token["hidden", t])
                        else:
                            act.wait(token["x", NT - 1, 1])
                        token["silu", t] = act.do(lambda e: e.activation(gated[:, t], bank[bk][:], ACT.Silu))
                        read_by(bk, token["silu", t])
                    else:
                        dve.wait(done, token["silu", t])
                        if ("hidden turned", t) in token:
                            dve.wait(token["hidden turned", t])
                        token["hidden", t] = dve.do(lambda e: e.tensor_tensor(hidden[:, t], bank[bk][:],
                                                                              gated[:, t], ALU.mult))
                        read_by(bk, token["hidden", t])
                    if s == 2:
                        turn_hidden(0, t)
                else:
                    kh = s - 4
                    done = []
                    for half, piece_slot in enumerate((t0, t1)):
                        if t == 0 and half:
                            pe.wait(*ready1)
                        done.append(rows_piece(hid, t, piece_slot, kh, DOWN_BANKS[t][half]))
                    if s == 4:
                        turn_hidden(1, t)
                        split_low(taken[0] + 2)
                        if t == 0 and follows:
                            turn_next(0)
                    else:
                        for half in range(2):
                            down_out(u, t, half, DOWN_BANKS[t][half], done[half])
            tile(0)
            split_low(taken[0] + 2)
            if s == 5 and follows:
                each_tile(u + 1, turn_next, first=1)
            each_tile(u, tile, first=1)
            last = [(s_, n) for s_, n in zip(pe.sems, pe.counts) if n]
            split_free[t0] = split_free[t1] = last

        def down_out(u, t, half, bk, done):
            cut = slice(half * HALF, (half + 1) * HALF)
            if u < SHARED:
                dve.wait(done)
                token["x", t, half] = dve.do(lambda e: e.tensor_tensor(x_rows[:, t, cut], bank[bk][:],
                                                                      x_rows[:, t, cut], ALU.add))
                read_by(bk, token["x", t, half])
            else:
                n = (u - SHARED) * NT + t
                act.wait(done, token["base"])
                if scattered[t].count:
                    act.wait((scattered[t].sem, scattered[t].count))
                token["y", t] = act.do(lambda e: e.activation(x_rows[:, t, cut], bank[bk][:], ACT.Copy,
                                                              scale=slot_w[:, n:n + 1]))
                read_by(bk, token["y", t])

        def scatter(x, t):
            n = x * NT + t
            pool.wait(token["y", t], token["base"])
            pool.wait(*((a.sem, a.count) for a in scattered if a.count))
            scattered[t].start(pool, lambda e: e.indirect_dma_start(
                out=out, out_offset=bass.IndirectOffsetOnAxis(ap=scatter_at[:, n:n + 1], axis=0),
                in_=x_rows[:, t, :], in_offset=None, compute_op=ALU.add))

        base_out = Arrival(sem("base_out"))
        for u in range(UNITS):
            x = u - SHARED
            for s in range(6):
                stage(u, s)
                if side:
                    side.pop(0)()
                if u == 0 and s == 4:
                    load_words()
                if s == 5 and u + 2 < UNITS:
                    each_tile(u + 2, lambda t: gather(x + 2, t))
            assert not side or u == 0
            if x >= 0:
                each_tile(u, lambda t: scatter(x, t))
            elif u == SHARED - 1:
                pool.wait(*(token["x", t, half] for t in range(NT) for half in range(2)))
                token["base"] = base_out.load(pool, out[0:N, :].rearrange("(t p) d -> p t d", p=P), x_rows[:])
                pool.wait(token["base"])
        assert taken[0] == len(pieces)

        sync.wait(*((a.sem, a.count) for a in scattered), token["base"], have_normed)

        block = ctx.enter_context(nc.Block())
        block.sync(sync.emit)
        block.gpsimd(pool.emit)
        block.scalar(act.emit)
        block.vector(dve.emit)
        block.tensor(pe.emit)


def kernel(**inputs):
    import concourse.bacc as bacc
    from concourse.bass_utils import run_bass_kernel_spmd

    def get(name):
        return np.ascontiguousarray(inputs[name])

    def columns(v):
        return np.ascontiguousarray(v.reshape(-1, P).T)

    arrays = {"x": get("x"), "src": get("src"), "dst": get("dst"),
              "src_cols": columns(get("src")), "dst_cols": columns(get("dst")),
              "type_cols": columns(get("edge_type_5")), "etw": get("L0_gnn_edge_type_weights")}
    for name in ("wq", "wk", "wv", "wiq", "wik", "wiv", "wo"):
        arrays[name] = np.ascontiguousarray(get("L0_gnn_" + name).T)
    for name in ("bq", "bk", "bv", "biq", "bik"):
        arrays[name] = columns(get("L0_gnn_" + name))
    arrays.update(biv=get("L0_gnn_biv"), bo=get("L0_gnn_bo"),
                  router=np.ascontiguousarray(get("L0_ffn_router_w").T), e_bias=get("L0_ffn_bias"),
                  gate=get("L0_ffn_gate_w"), up=get("L0_ffn_up_w"), down=get("L0_ffn_down_w"),
                  sh_gate=get("L0_ffn_sh_gate_w"), sh_up=get("L0_ffn_sh_up_w"),
                  sh_down=get("L0_ffn_sh_down_w"))

    nc = bacc.Bacc("TRN2", target_bir_lowering=False, num_devices=1)
    aps = {name: nc.dram_tensor("in_" + name, a.shape, mybir.dt.from_np(a.dtype), kind="ExternalInput").ap()
           for name, a in arrays.items()}
    normed = nc.dram_tensor("normed", (N, D), F32, kind="Internal").ap()
    out = nc.dram_tensor("result", (N + P, D), F32, kind="ExternalOutput").ap()
    build(nc, aps, normed, out)
    ran = run_bass_kernel_spmd(nc, [{"in_" + name: a for name, a in arrays.items()}], core_ids=[0])
    return ran.results[0]["result"][:N]
```
